# Optimizing a Trainium2 kernel written in Bass

```python
import numpy as np
import jax
import jax.numpy as jnp

def _softmax(x, axis=-1):
    return jax.nn.softmax(x, axis=axis)

def _gelu(x):
    return jax.nn.gelu(x, approximate=True)

def _silu(x):
    return jax.nn.silu(x)

def _sigmoid(x):
    return jax.nn.sigmoid(x)

def _layernorm(x, axis=-1, eps=1e-05):
    m = jnp.mean(x, axis=axis, keepdims=True)
    v = jnp.var(x, axis=axis, keepdims=True)
    return (x - m) / jnp.sqrt(v + eps)

def _scatter_add(tgt, idx, src, axis=0):
    return tgt.at[idx].add(src)

def _segment_sum(src, seg, n):
    return jax.ops.segment_sum(src, seg, n)
kernel_name = 'mk_gnn_ffn_d1_gnn_r32_30d5a1'

def setup_inputs(seed: int=0):
    np.random.seed(seed)
    _w = jnp.asarray

    def _rec_inputs():
        import jax
        import jax.numpy as jnp
        _gk = jax.random.key(seed)
        x = -0.0002117 + 1 * jax.random.normal(jax.random.fold_in(_gk, 1), (3125, 256), jnp.float32)
        _s = jax.random.randint(jax.random.fold_in(_gk, 2), (25000,), 0, 3125, jnp.int32)
        _d = jax.random.randint(jax.random.fold_in(_gk, 3), (25000,), 0, 3125, jnp.int32)
        _loop = jnp.arange(3125, dtype=jnp.int32)
        src = jnp.concatenate([_s, _d, _loop])
        dst = jnp.concatenate([_d, _s, _loop])
        _o = jnp.argsort(dst, stable=True)
        src = src[_o]
        dst = dst[_o]
        edge_weight = jax.random.uniform(jax.random.fold_in(_gk, 12), (53125,), jnp.float32, 0.0, 1)
        return (x, src, dst, edge_weight)
    x, src, dst, edge_weight = _rec_inputs()

    def _L0_gnn_setup():
        import jax, jax.numpy as jnp
        import numpy as np
        N = 3125
        E = 50000
        D_IN = 256
        D_OUT = 256
        NEG_SLOPE = 0.01
        key = jax.random.key(seed)
        k1, k2, k3, k4, k5, k6 = jax.random.split(key, 6)
        ego_embeddings = jax.random.normal(k1, (N, D_IN), dtype=jnp.float32)
        rows = jax.random.randint(k2, (E,), 0, N, dtype=jnp.int32)
        cols = jax.random.randint(k3, (E,), 0, N, dtype=jnp.int32)
        vals = jax.random.uniform(k4, (E,), dtype=jnp.float32)
        W1 = jax.random.normal(k5, (D_IN, D_OUT), dtype=jnp.float32) * (1.0 / np.sqrt(D_IN))
        W2 = jax.random.normal(k6, (D_IN, D_OUT), dtype=jnp.float32) * (1.0 / np.sqrt(D_IN))
        b1 = jnp.zeros((D_OUT,), dtype=jnp.float32)
        b2 = jnp.zeros((D_OUT,), dtype=jnp.float32)
        return {'ego_embeddings': ego_embeddings, 'vals': vals, 'W1': W1, 'b1': b1, 'W2': W2, 'b2': b2, 'rows': rows, 'cols': cols}
    _L0_gnn_all = _L0_gnn_setup()
    _L0_gnn_in = {k: v for k, v in _L0_gnn_all.items() if k in ('W1', 'b1', 'W2', 'b2')}
    del _L0_gnn_all

    def _L0_ffn_setup():
        import jax, jax.numpy as jnp
        import numpy as np
        B, S, D = (8, 128, 256)
        H = 4 * D
        CAPACITY = 0.5
        key = jax.random.key(seed)
        ks = jax.random.split(key, 6)
        x = jax.random.normal(ks[0], (B, S, D), dtype=jnp.float32)
        attention_mask = jnp.zeros((B, 1, 1, S), dtype=jnp.float32)
        wr = jax.random.normal(ks[1], (D, 1), dtype=jnp.float32) * 0.02
        br = jnp.zeros((1,), dtype=jnp.float32)
        w1 = jax.random.normal(ks[2], (D, H), dtype=jnp.float32) * 0.02
        b1 = jnp.zeros((H,), dtype=jnp.float32)
        w2 = jax.random.normal(ks[3], (H, D), dtype=jnp.float32) * 0.02
        b2 = jnp.zeros((D,), dtype=jnp.float32)
        return {'x': x, 'attention_mask': attention_mask, 'wr': wr, 'br': br, 'w1': w1, 'b1': b1, 'w2': w2, 'b2': b2}
    _L0_ffn_all = _L0_ffn_setup()
    _L0_ffn_in = {k: v for k, v in _L0_ffn_all.items() if k in ('attention_mask', 'wr', 'br', 'w1', 'b1', 'w2', 'b2')}
    del _L0_ffn_all
    return {'x': x, 'src': src, 'dst': dst, 'edge_weight': edge_weight, 'L0_gnn_W1': _L0_gnn_in['W1'], 'L0_gnn_b1': _L0_gnn_in['b1'], 'L0_gnn_W2': _L0_gnn_in['W2'], 'L0_gnn_b2': _L0_gnn_in['b2'], 'L0_ffn_attention_mask': _L0_ffn_in['attention_mask'], 'L0_ffn_wr': _L0_ffn_in['wr'], 'L0_ffn_br': _L0_ffn_in['br'], 'L0_ffn_w1': _L0_ffn_in['w1'], 'L0_ffn_b1': _L0_ffn_in['b1'], 'L0_ffn_w2': _L0_ffn_in['w2'], 'L0_ffn_b2': _L0_ffn_in['b2']}

def reference(x, src, dst, edge_weight, L0_gnn_W1, L0_gnn_b1, L0_gnn_W2, L0_gnn_b2, L0_ffn_attention_mask, L0_ffn_wr, L0_ffn_br, L0_ffn_w1, L0_ffn_b1, L0_ffn_w2, L0_ffn_b2):
    import jax
    import jax.numpy as jnp

    def _L0_gnn_ref(ego_embeddings, vals, W1, b1, W2, b2, rows, cols):
        import jax, jax.numpy as jnp
        import numpy as np
        N = 3125
        E = 50000
        D_IN = 256
        D_OUT = 256
        NEG_SLOPE = 0.01
        msgs = vals[:, None] * ego_embeddings[cols]
        side = jax.ops.segment_sum(msgs, rows, num_segments=N)
        sum_emb = jax.nn.leaky_relu((ego_embeddings + side) @ W1 + b1, NEG_SLOPE)
        bi_emb = jax.nn.leaky_relu(ego_embeddings * side @ W2 + b2, NEG_SLOPE)
        return sum_emb + bi_emb

    def _L0_ffn_ref(x, attention_mask, wr, br, w1, b1, w2, b2):
        import jax, jax.numpy as jnp
        import numpy as np
        B, S, D = (8, 128, 256)
        H = 4 * D
        CAPACITY = 0.5
        b, s, d = x.shape
        weights = (jnp.einsum('bsd,do->bso', x, wr) + br)[..., 0]
        k = max(1, int(CAPACITY * s))
        kk = k - 1 if k > 1 else 1
        _, idx = jax.lax.top_k(weights, k)
        sel_idx = idx[:, :kk]
        sel = jnp.take_along_axis(x, sel_idx[:, :, None], axis=1)
        h = jax.nn.gelu(jnp.einsum('bkd,dh->bkh', sel, w1) + b1)
        y = jnp.einsum('bkh,hd->bkd', h, w2) + b2
        w_sel = jnp.take_along_axis(weights, sel_idx, axis=1)
        y = y * w_sel[..., None]
        batch_idx = jnp.arange(b)[:, None]
        processed = jnp.zeros_like(x).at[batch_idx, sel_idx].set(y)
        return processed + x
    x = x + _L0_gnn_ref(_layernorm(x, axis=-1), edge_weight, L0_gnn_W1, L0_gnn_b1, L0_gnn_W2, L0_gnn_b2, src, dst)
    x = x + _L0_ffn_ref(_layernorm(x, axis=-1)[None], L0_ffn_attention_mask, L0_ffn_wr, L0_ffn_br, L0_ffn_w1, L0_ffn_b1, L0_ffn_w2, L0_ffn_b2)[0]
    return x

_drawn_inputs = setup_inputs


def setup_inputs(seed=0):
    import zlib

    import numpy as np

    out = dict(_drawn_inputs(seed))
    spreads = {'L0_gnn_b1': (0.0, 0.314),
     'L0_gnn_b2': (0.0, 0.303),
     'L0_ffn_b1': (0.0, 0.8),
     'L0_ffn_b2': (0.0, 0.8)}
    factors = {'L0_ffn_wr': 7.605, 'L0_ffn_w1': 8.0, 'L0_ffn_w2': 8.0}
    for name, (base, spread) in spreads.items():
        noise = np.random.default_rng([zlib.crc32(name.encode()), seed]).standard_normal(out[name].shape)
        drawn = base * np.exp(spread * noise) if base else spread * noise
        out[name] = jnp.asarray(drawn.astype(out[name].dtype))
    for name, factor in factors.items():
        out[name] = (out[name] * factor).astype(out[name].dtype)
    return out
```

```python
import concourse.bass as bass
from concourse import mybir
from contextlib import ExitStack

P = 128
N = 3125
D = 256
E = 53125
H = 1024
NB = -(-N // P)
NP = NB * P
KEEP = max(1, int(0.5 * N)) - 1
QT = -(-KEEP // P)
NCH = 5
TC = 84
assert NCH * TC * P >= E and TC % 12 == 0 and TC % 2 == 0
STEPS = TC + NB - 1
assert STEPS % 12 == 0 and STEPS <= P
RING = TC // 2
U = 12
NS = 6
NG = TC // U
SG = STEPS // U
EPS = 1e-5
BIG = 3.0e38
XP = 5
XB = NB // XP



def build(nc, x, src, dst, w_edge, W1, b1, W2, b2, wr, br, fw1, fb1, fw2, fb2, out):
    f32 = mybir.dt.float32
    i32 = mybir.dt.int32
    bf16 = mybir.dt.bfloat16
    ALU = mybir.AluOpType
    ACT = mybir.ActivationFunctionType
    AX = mybir.AxisListType
    DVE = [mybir.EngineType.DVE]
    PE = [mybir.EngineType.PE]

    ctx = ExitStack()
    with ctx:
        def sb(name, shape, dt=f32):
            return ctx.enter_context(nc.sbuf_tensor(name, shape, dt))

        def sem(name):
            return ctx.enter_context(nc.semaphore(name))

        ego_rows = nc.dram_tensor("ego_rows", [NP, D], f32, kind="Internal").ap()
        xn2_rows = nc.dram_tensor("xn2_rows", [NP, D], f32, kind="Internal").ap()
        base_rows = nc.dram_tensor("base_rows", [NP, D], f32, kind="Internal").ap()

        X = sb("X", [P, NB, D])
        EGO = sb("EGO", [P, NB, D])
        SIDE = sb("SIDE", [P, NB + 1, D])
        ROWS = sb("ROWS", [P, RING * D])
        EDGE_SRC = sb("EDGE_SRC", [P, NCH * TC], i32)
        EDGE_DST = sb("EDGE_DST", [P, NCH * TC], i32)
        EDGE_W = sb("EDGE_W", [P, NCH * TC])
        OH = sb("OH", [P, NB * TC], bf16)
        CNT = sb("CNT", [P, NB * TC])
        IOTA = sb("IOTA", [P, (NB + 1) * P])
        IDENT = sb("IDENT", [P, P])
        LOWER = sb("LOWER", [P, P])
        BELOW = sb("BELOW", [P, P])
        ONES = sb("ONES", [P, P])
        PIDX = sb("PIDX", [P, 1])
        W1S = sb("W1S", [P, 2, D])
        W2S = sb("W2S", [P, 2, D])
        BROW = sb("BROW", [1, 3, D])
        FW1 = sb("FW1", [P, 2, H])
        FB1 = sb("FB1", [P, H // P])
        FW2 = sb("FW2", [P, H // P, D])
        WRB = sb("WRB", [P, D])
        BRB = sb("BRB", [P, 1])
        BLK = sb("BLK", [P, TC], i32)
        POSF = sb("POSF", [P, TC])
        POSI = sb("POSI", [P, TC], i32)
        QR = sb("QR", [P, 2, TC], i32)
        QRF = sb("QRF", [P, 2, TC])
        KEYF = sb("KEYF", [P, TC])
        CX = sb("CX", [P, NB + 1])
        NCNT = sb("NCNT", [P, NB])
        BASE = sb("BASE", [P, NB])
        SM_I = sb("SM_I", [P, 4, NB + 1], i32)
        SM_F = sb("SM_F", [P, 8, NB + 1])
        STEPV = sb("STEPV", [P, 8])
        TAB = sb("TAB", [1, 2, 3, STEPS], i32)
        TABP = sb("TABP", [1, 2, STEPS], i32)
        PSEL = sb("PSEL", [P, 4, P])
        PVAL = sb("PVAL", [P, 4, 2 * TC])
        SKEY = sb("SKEY", [P, TC], i32)
        SHI = sb("SHI", [P, TC], i32)
        SDST = sb("SDST", [P, 2, TC], i32)
        SSRC = sb("SSRC", [P, 2, TC])
        SW = sb("SW", [P, 2, TC])
        SEL = sb("SEL", [P, 4, P])
        STAT = sb("STAT", [P, NB, 6])
        MV = sb("MV", [P, NB, 2])
        RS = sb("RS", [P, 4, NB])
        WT = sb("WT", [P, NB])

        perm_ps = ctx.enter_context(nc.psum_tensor("perm_ps", [P, 512], f32))
        step_ps = [ctx.enter_context(nc.psum_tensor(f"step_ps{i}", [P, 512], f32)) for i in range(2)]
        small_ps = ctx.enter_context(nc.psum_tensor("small_ps", [P, 512], f32))
        wide_ps = [ctx.enter_context(nc.psum_tensor(f"wide_ps{i}", [P, 512], f32)) for i in range(4)]

        def step_out(k):
            return (*step_ps, *wide_ps[0:2])[k % 4][:, 0:D]

        s_edges = sem("s_edges")
        s_xin = [sem(f"s_xin{i}") for i in range(XP)]
        s_wts = sem("s_wts")
        s_const = sem("s_const")
        s_pool_seen = sem("s_pool_seen")
        s_pe_seen = sem("s_pe_seen")
        s_pool = sem("s_pool")
        s_var = sem("s_var")
        s_std = sem("s_std")
        s_ego = sem("s_ego")
        s_mixT_mm = sem("s_mixT_mm")
        s_mixT = sem("s_mixT")
        s_ego_dram = sem("s_ego_dram")
        s_dve = sem("s_dve")
        s_hist = sem("s_hist")
        s_base = sem("s_base")
        s_stepv = sem("s_stepv")
        s_tabmm = sem("s_tabmm")
        s_tab = sem("s_tab")
        s_perm = sem("s_perm")
        s_perm_used = sem("s_perm_used")
        s_sorted = sem("s_sorted")
        s_gather = [sem(f"s_gather{i}") for i in range(NS)]
        s_sel = sem("s_sel")
        s_step = sem("s_step")
        s_added = sem("s_added")
        s_mixs = sem("s_mixs")
        s_mixp = sem("s_mixp")
        s_gnn = sem("s_gnn")
        s_relu = sem("s_relu")
        s_leak = sem("s_leak")
        s_x2 = sem("s_x2")
        s_var2 = sem("s_var2")
        s_std2 = sem("s_std2")
        s_xn2 = sem("s_xn2")
        s_sum2 = sem("s_sum2")
        s_tok_dram = sem("s_tok_dram")
        s_base_dram = sem("s_base_dram")
        s_wt = sem("s_wt")
        s_wrow_mm = sem("s_wrow_mm")
        s_wrow = sem("s_wrow")
        s_rank = sem("s_rank")
        s_rank_mm = sem("s_rank_mm")
        s_pack = sem("s_pack")
        s_pack_used = sem("s_pack_used")
        s_kept = sem("s_kept")
        s_tokens = [sem(f"s_tokens{i}") for i in range(4)]
        s_bases = [sem(f"s_bases{i}") for i in range(4)]
        s_tokT_mm = sem("s_tokT_mm")
        s_tokT = sem("s_tokT")
        s_h_mm = sem("s_h_mm")
        s_h = sem("s_h")
        s_y_mm = sem("s_y_mm")
        s_y = sem("s_y")
        s_out = sem("s_out")

        XN2 = EGO
        BASE2 = SIDE[:, 0:NB, :]
        XFLAT = X[:, :, :].rearrange("p b d -> p (b d)")
        WROW = XFLAT[:, 0:NP]
        CMP = XFLAT[:, NP:2 * NP]
        TOK = ROWS[:, 0:8 * D]
        TOKT = ROWS[:, 8 * D:16 * D]
        HT = ROWS[:, 16 * D:32 * D].rearrange("p (k n) -> p k n", k=H // P)
        TBASE = ROWS[:, 32 * D:40 * D]
        YOUT = XFLAT[:, 0:8 * D]
        MIX = ROWS[:, 0:8 * D].rearrange("p (k m d) -> p k m d", k=4, m=2)
        MIXT = ROWS[:, 8 * D:12 * D].rearrange("p (k a n) -> p k a n", k=2, a=4)
        RELU = ROWS[:, 12 * D:16 * D].rearrange("p (k d) -> p k d", k=2)
        SCR = ROWS[:, 16 * D:(16 + XB) * D]
        RANK = sb("RANK", [P, NB, 3])
        CMPT = sb("CMPT", [P, P])
        NODE = sb("NODE", [P, NB])
        SLOT = sb("SLOT", [P, QT])
        KEPT = sb("KEPT", [P, QT], i32)
        KEPTO = sb("KEPTO", [P, QT], i32)
        KEPTW = sb("KEPTW", [P, QT])
        KF = sb("KF", [P, 3, NB])
        KI = sb("KI", [P, 3, NB], i32)
        KQR = sb("KQR", [P, 2, NB])

        GROUPS = [list(range(q, min(q + 4, QT))) for q in range(0, QT, 4)]

        block = ctx.enter_context(nc.Block())

        @block.sync
        def _(sp):
            xv = x.rearrange("(b p) d -> p b d", p=P)
            sp.dma_start(X[:, 0:XB, :], xv[:, 0:XB, :]).then_inc(s_xin[0], 16)
            sp.dma_start(EDGE_SRC[:, :], src).then_inc(s_edges, 16)
            sp.dma_start(EDGE_DST[:, :], dst).then_inc(s_edges, 16)
            sp.dma_start(EDGE_W[:, :], w_edge).then_inc(s_edges, 16)
            for i in range(1, XP):
                sp.dma_start(X[:, i * XB:(i + 1) * XB, :], xv[:, i * XB:(i + 1) * XB, :]).then_inc(s_xin[i], 16)
            sp.dma_start(W1S[:, :, :], W1.rearrange("(k p) n -> p k n", p=P)).then_inc(s_wts, 16)
            sp.dma_start(W2S[:, :, :], W2.rearrange("(k p) n -> p k n", p=P)).then_inc(s_wts, 16)
            sp.dma_start(BROW[:, 0, :], b1.rearrange("(a n) -> a n", a=1)).then_inc(s_wts, 16)
            sp.dma_start(BROW[:, 1, :], b2.rearrange("(a n) -> a n", a=1)).then_inc(s_wts, 16)
            sp.dma_start(BROW[:, 2, :], fb2.rearrange("(a n) -> a n", a=1)).then_inc(s_wts, 16)
            sp.dma_start(FW1[:, :, :], fw1.rearrange("(k p) n -> p k n", p=P)).then_inc(s_wts, 16)
            sp.dma_start(FW2[:, :, :], fw2.rearrange("(k p) n -> p k n", p=P)).then_inc(s_wts, 16)
            sp.dma_start(FB1[:, :], fb1).then_inc(s_wts, 16)
            sp.dma_start(WRB[:, :], bass.AP(tensor=wr.tensor, offset=0, ap=[[0, P], [1, D]])).then_inc(s_wts, 16)
            sp.dma_start(BRB[:, :], bass.AP(tensor=br.tensor, offset=0, ap=[[0, P], [1, 1]])).then_inc(s_wts, 16)
            ev = ego_rows.rearrange("(b p) d -> p b d", p=P)
            for i in range(XP):
                sp.wait_ge(s_ego, i + 1)
                sp.dma_start(ev[:, i * XB:(i + 1) * XB, :], EGO[:, i * XB:(i + 1) * XB, :]).then_inc(s_ego_dram, 16)
            nv = xn2_rows.rearrange("(b p) d -> p b d", p=P)
            ov = out.rearrange("(b p) d -> p b d", p=P)
            bv = base_rows.rearrange("(b p) d -> p b d", p=P)
            for i in range(XP):
                part = slice(i * XB, (i + 1) * XB)
                sp.wait_ge(s_xn2, i + 1)
                sp.dma_start(nv[:, part, :], XN2[:, part, :]).then_inc(s_tok_dram, 16)
                sp.wait_ge(s_sum2, i + 1)
                sp.dma_start(bv[:, part, :], BASE2[:, part, :]).then_inc(s_tok_dram, 16)
                sp.dma_start(ov[:, part, :], BASE2[:, part, :]).then_inc(s_base_dram, 16)
            sp.wait_ge(s_ego_dram, 16 * XP)
            sp.wait_ge(s_tok_dram, 32 * XP)
            sp.wait_ge(s_base_dram, 16 * XP)
            sp.wait_ge(s_out, 16 * QT)

        def mix_sum(pool, b, k):
            pool.tensor_tensor(MIX[:, k, 0, :], EGO[:, bass.ds(b, 1), :].rearrange("p a d -> p (a d)"),
                               SIDE[:, bass.ds(b, 1), :].rearrange("p a d -> p (a d)"), ALU.add).then_inc(s_mixs, 1)

        @block.gpsimd
        def _(pool):
            pool.iota(IOTA[:, :], pattern=[[1, (NB + 1) * P]], base=0, channel_multiplier=0,
                      allow_small_or_imprecise_dtypes=True).then_inc(s_const, 1)
            pool.iota(PIDX[:, :], pattern=[[0, 1]], base=0, channel_multiplier=1,
                      allow_small_or_imprecise_dtypes=True).then_inc(s_const, 1)
            pool.iota(NODE[:, :], pattern=[[P, NB]], base=0, channel_multiplier=1,
                      allow_small_or_imprecise_dtypes=True).then_inc(s_const, 1)
            pool.iota(SLOT[:, :], pattern=[[P, QT]], base=0, channel_multiplier=1,
                      allow_small_or_imprecise_dtypes=True).then_inc(s_const, 1)
            pool.memset(IDENT[:, :], 0.0).then_inc(s_pool, 1)
            pool.memset(ONES[:, :], 1.0).then_inc(s_pool, 1)
            pool.wait_ge(s_pool, 2)
            pool.affine_select(out=IDENT[:, :], in_=IDENT[:, :], compare_op=ALU.not_equal, fill=1.0,
                               base=0, pattern=[[-1, P]], channel_multiplier=1).then_inc(s_const, 1)
            pool.affine_select(out=LOWER[:, :], in_=ONES[:, :], compare_op=ALU.is_gt, fill=0.0,
                               base=0, pattern=[[1, P]], channel_multiplier=-1).then_inc(s_const, 1)
            pool.affine_select(out=BELOW[:, :], in_=ONES[:, :], compare_op=ALU.is_gt, fill=0.0,
                               base=0, pattern=[[-1, P]], channel_multiplier=1).then_inc(s_const, 1)
            pool.memset(SIDE[:, :, :], 0.0).then_inc(s_const, 1)

            def gathers(c, par, first=False):
                pool.wait_ge(s_sorted, c + 1)
                for j in range(TC):
                    if j >= RING:
                        pool.wait_ge(s_step, c * STEPS + j - RING + NB)
                    elif not first:
                        pool.wait_ge(s_step, (c - 1) * STEPS + j + RING + NB)
                    if not first or j >= NS:
                        pool.wait_ge(s_gather[j % NS], (c * (TC // NS) + j // NS) * 16)
                    pool.sem_inc(s_pool_seen, 1)
                    s = j % RING
                    pool.indirect_dma_start(
                        out=ROWS[:, s * D:(s + 1) * D], out_offset=None, in_=ego_rows,
                        in_offset=bass.IndirectOffsetOnAxis(ap=SDST[:, par, j:j + 1], axis=0),
                    ).then_inc(s_gather[j % NS], 16)

            pool.wait_ge(s_ego_dram, 16 * XP)
            gathers(0, 0, first=True)
            with pool.Fori(0, (NCH - 1) // 2) as i:
                gathers(i * 2 + 1, 1)
                gathers(i * 2 + 2, 0)

            pool.wait_ge(s_added, NCH * STEPS)
            for b in range(4):
                mix_sum(pool, b, b)
            with pool.Fori(1, NB // 4) as i:
                for k in range(4):
                    pool.wait_ge(s_mixT_mm, i * 4 + k - 3)
                    mix_sum(pool, i * 4 + k, k)
            pool.wait_ge(s_mixT_mm, NB - 4)
            mix_sum(pool, NB - 1, 0)

            with pool.Fori(0, XP) as i:
                pool.wait_ge(s_xn2, i + 1)
                pool.tensor_tensor(BASE2[:, bass.ds(i * XB, XB), :], X[:, bass.ds(i * XB, XB), :],
                                   XN2[:, bass.ds(i * XB, XB), :], ALU.add).then_inc(s_sum2, 1)

            def store_kept(q):
                pool.wait_ge(s_y, q + 1)
                pool.indirect_dma_start(
                    out=out, out_offset=bass.IndirectOffsetOnAxis(ap=KEPTO[:, q:q + 1], axis=0),
                    in_=YOUT[:, (q % 8) * D:(q % 8 + 1) * D], in_offset=None,
                    bounds_check=NP - 1, oob_is_err=False).then_inc(s_out, 16)

            pool.wait_ge(s_kept, 1)
            pool.wait_ge(s_tok_dram, 32 * XP)
            pool.wait_ge(s_base_dram, 16 * XP)
            for g, tiles in enumerate(GROUPS):
                for q in tiles:
                    s = q % 8
                    if q >= 8:
                        pool.wait_ge(s_tokT_mm, (q - 8) // 2 + 1)
                        pool.wait_ge(s_y, q - 7)
                    if q >= 4:
                        pool.wait_ge(s_tokens[q % 4], 16 * (q // 4))
                        pool.wait_ge(s_bases[q % 4], 16 * (q // 4))
                    pool.indirect_dma_start(
                        out=TOK[:, s * D:(s + 1) * D], out_offset=None, in_=xn2_rows,
                        in_offset=bass.IndirectOffsetOnAxis(ap=KEPT[:, q:q + 1], axis=0),
                    ).then_inc(s_tokens[q % 4], 16)
                    pool.indirect_dma_start(
                        out=TBASE[:, s * D:(s + 1) * D], out_offset=None, in_=base_rows,
                        in_offset=bass.IndirectOffsetOnAxis(ap=KEPT[:, q:q + 1], axis=0),
                    ).then_inc(s_bases[q % 4], 16)
                if g >= 1:
                    for q in GROUPS[g - 1]:
                        store_kept(q)
            for q in GROUPS[-1]:
                store_kept(q)

        @block.scalar
        def _(act):
            for i in range(XP):
                act.wait_ge(s_var, i + 1)
                act.activation(RS[:, 1, i * XB:(i + 1) * XB], RS[:, 0, i * XB:(i + 1) * XB], ACT.Sqrt).then_inc(s_std, 1)
            def copy_mix(b, k, first=False):
                act.wait_ge(s_mixT_mm, b + 1)
                if not first:
                    act.wait_ge(s_gnn, b - 1)
                act.activation(MIXT[:, k % 2, :, :].rearrange("p a n -> p (a n)"), step_ps[k % 2][:, :],
                               ACT.Copy).then_inc(s_mixT, 1)

            def relus(b, k, first=False):
                act.wait_ge(s_gnn, b + 1)
                if not first:
                    act.wait_ge(s_x2, b - 1)
                act.activation(RELU[:, k % 2, :], wide_ps[k % 2][:, :], ACT.Copy, scale=0.01).then_inc(s_relu, 1)

            copy_mix(0, 0, True)
            for b in range(4):
                copy_mix(b + 1, b + 1, b < 1)
                relus(b, b, b < 2)
            with act.Fori(1, NB // 4) as i:
                for k in range(4):
                    copy_mix(i * 4 + k + 1, k + 1)
                    relus(i * 4 + k, k)
            relus(NB - 1, 0)
            act.wait_ge(s_var2, 1)
            act.activation(RS[:, 1, :], RS[:, 0, :], ACT.Sqrt).then_inc(s_std2, 1)
            act.wait_ge(s_sum2, XP)
            for i in range(-(-NB // 4)):
                n = min(4, NB - 4 * i)
                act.wait_ge(s_wrow_mm, i + 1)
                act.activation(WROW[:, i * 512:i * 512 + n * P], wide_ps[i % 4][:, 0:n * P], ACT.Copy).then_inc(s_wrow, 1)
            pair = 0
            for g, tiles in enumerate(GROUPS):
                for j in range(0, len(tiles), 2):
                    n = min(2, len(tiles) - j)
                    act.wait_ge(s_tokT_mm, pair + 1)
                    if g >= 2 and j == 0:
                        act.wait_ge(s_y_mm, GROUPS[g - 2][-1] + 1)
                    tokt = TOKT[:, (g % 2) * 4 * D:(g % 2 + 1) * 4 * D].rearrange("p (h n) -> p h n", h=2)
                    act.activation(tokt[:, :, j * P:(j + n) * P],
                                   step_ps[pair % 2][:, :].rearrange("p (h n) -> p h n", h=2)[:, :, 0:n * P],
                                   ACT.Copy).then_inc(s_tokT, 1)
                    pair += 1
                n = len(tiles) * P
                for k in range(H // P):
                    act.wait_ge(s_h_mm, g * (H // P) + k + 1)
                    if g >= 1 and k == 0:
                        act.wait_ge(s_y_mm, GROUPS[g - 1][-1] + 1)
                    act.activation(HT[:, k, 0:n], wide_ps[k % 2][:, 0:n], ACT.Gelu_apprx_tanh,
                                   bias=FB1[:, k:k + 1]).then_inc(s_h, 1)

        @block.vector
        def _(dve):
            chain = {"base": 0, "n": 0}

            def link(ins):
                chain["n"] += 1
                ins.then_inc(s_dve, 1)
                dve.wait_ge(s_dve, chain["base"] + chain["n"])

            def rsqrt_newton(v, s, y, t):
                link(nc.vector.reciprocal(y, s))
                link(nc.vector.tensor_tensor(t, y, y, ALU.mult))
                link(nc.vector.tensor_tensor(t, t, v, ALU.mult))
                link(nc.vector.tensor_scalar(t, t, -0.5, 1.5, ALU.mult, ALU.add))
                link(nc.vector.tensor_tensor(y, y, t, ALU.mult))

            for i in range(XP):
                part = slice(i * XB, (i + 1) * XB)
                dve.wait_ge(s_xin[i], 16)
                for b in range(i * XB, (i + 1) * XB):
                    last = nc.vector.bn_stats(STAT[:, b, :], X[:, b, :])
                link(last)
                for b in range(i * XB, (i + 1) * XB):
                    last = nc.vector.bn_aggr(MV[:, b, :], STAT[:, b, :])
                link(last)
                nc.vector.tensor_scalar(RS[:, 0, part], MV[:, part, 1], EPS, None, ALU.add).then_inc(s_var, 1)
                dve.wait_ge(s_std, i + 1)
                rsqrt_newton(RS[:, 0, part], RS[:, 1, part], RS[:, 2, part], RS[:, 3, part])
                for b in range(i * XB, (i + 1) * XB):
                    last = nc.vector.tensor_scalar(EGO[:, b, :], X[:, b, :], MV[:, b, 0:1], RS[:, 2, b:b + 1],
                                                   ALU.subtract, ALU.mult)
                last.then_inc(s_ego, 1)
            ln_links = chain["n"]

            oh = OH[:, :].rearrange("p (b t) -> p b t", b=NB)
            cnt = CNT[:, :].rearrange("p (b t) -> p b t", b=NB)

            def sort(c, par):
                start = chain["n"]
                e_src = EDGE_SRC[:, bass.ds(c * TC, TC)]
                e_dst = EDGE_DST[:, bass.ds(c * TC, TC)]
                nc.vector.scalar_tensor_tensor(KEYF[:, :], e_src, 4096.0, e_dst, ALU.mult, ALU.add)
                link(nc.vector.tensor_scalar(BLK[:, :], e_src, 7, None, ALU.logical_shift_right))
                link(nc.vector.tensor_tensor(oh, BLK[:, :].unsqueeze(1).to_broadcast([P, NB, TC]),
                                             IOTA[:, 0:NB].unsqueeze(2).to_broadcast([P, NB, TC]), ALU.is_equal))
                link(nc.vector.tensor_tensor_scan(CNT[:, :], OH[:, :], OH[:, :], 0.0, ALU.add, ALU.max))
                link(nc.vector.tensor_copy(CX[:, 1:NB + 1], cnt[:, :, TC - 1]))
                nc.vector.tensor_tensor(NCNT[:, :], CX[:, 1:NB + 1], CX[:, 0:NB], ALU.subtract).then_inc(s_hist, 1)
                dve.wait_ge(s_base, c + 1)
                link(nc.vector.scalar_tensor_tensor(BASE[:, :], small_ps[:, 0:NB], -1.0, CX[:, 0:NB],
                                                    ALU.add, ALU.subtract))
                nc.vector.tensor_copy(SM_F[:, 0, :], small_ps[:, 32:32 + NB + 1])
                link(nc.vector.tensor_copy(SM_I[:, 0, :], small_ps[:, 32:32 + NB + 1]))
                link(nc.vector.tensor_tensor(cnt, cnt, BASE[:, :].unsqueeze(2).to_broadcast([P, NB, TC]), ALU.add))
                link(nc.vector.tensor_tensor(CNT[:, :], CNT[:, :], OH[:, :], ALU.mult))
                link(nc.vector.tensor_reduce(POSF[:, :], cnt.rearrange("p b t -> p t b"), AX.X, ALU.add))
                link(nc.vector.tensor_copy(POSI[:, :], POSF[:, :]))
                nc.vector.tensor_scalar(QR[:, 0, :], POSI[:, :], 7, None, ALU.logical_shift_right)
                link(nc.vector.tensor_scalar(QR[:, 1, :], POSI[:, :], P - 1, None, ALU.bitwise_and))
                link(nc.vector.tensor_copy(QRF[:, :, :], QR[:, :, :]))
                nc.vector.tensor_scalar(SM_I[:, 1, :], SM_I[:, 0, :], 7, None, ALU.logical_shift_right)
                link(nc.vector.tensor_scalar(SM_I[:, 2, :], SM_I[:, 0, :], P - 1, None, ALU.add))
                link(nc.vector.tensor_scalar(SM_I[:, 3, :], SM_I[:, 2, :], 7, None, ALU.logical_shift_right))
                nc.vector.tensor_tensor(SM_F[:, 1, 0:NB], SM_I[:, 3, 1:NB + 1], SM_I[:, 1, 0:NB], ALU.subtract)
                link(nc.vector.tensor_tensor(SM_F[:, 2, 0:NB], SM_F[:, 0, 1:NB + 1], SM_F[:, 0, 0:NB], ALU.is_gt))
                link(nc.vector.tensor_tensor(SM_F[:, 3, 0:NB], SM_F[:, 1, 0:NB], SM_F[:, 2, 0:NB], ALU.mult))
                link(nc.vector.tensor_tensor_scan(SM_F[:, 4, 0:NB], SM_F[:, 3, 0:NB], SM_F[:, 3, 0:NB], 0.0,
                                                  ALU.add, ALU.max))
                link(nc.vector.tensor_tensor(SM_F[:, 5, 0:NB], SM_I[:, 1, 0:NB], SM_F[:, 4, 0:NB], ALU.subtract))
                nc.vector.tensor_tensor(SM_F[:, 6, 0:NB], SM_F[:, 5, 0:NB], SM_F[:, 3, 0:NB], ALU.add)
                link(nc.vector.tensor_scalar(SM_F[:, 7, 0:NB], SM_F[:, 4, 0:NB], PIDX[:, 0:1], 0.0, ALU.is_le, ALU.add,
                                             accum_out=STEPV[:, 3:4]))
                link(nc.vector.scalar_tensor_tensor(SM_F[:, 5, 0:NB], IOTA[:, 0:NB], STEPV[:, 3:4], SM_F[:, 6, 0:NB],
                                                    ALU.is_equal, ALU.mult, accum_out=STEPV[:, 4:5]))
                nc.vector.tensor_scalar(STEPV[:, 1:2], STEPV[:, 3:4], float(P), None, ALU.mult)
                link(nc.vector.tensor_scalar(STEPV[:, 5:6], STEPV[:, 4:5], PIDX[:, 0:1], None, ALU.add))
                link(nc.vector.tensor_scalar(STEPV[:, 0:1], STEPV[:, 5:6], float(TC - 1), None, ALU.min))
                link(nc.vector.tensor_scalar(STEPV[:, 6:7], STEPV[:, 0:1], float(RING), -float(RING), ALU.is_ge, ALU.mult))
                link(nc.vector.tensor_tensor(STEPV[:, 7:8], STEPV[:, 6:7], STEPV[:, 0:1], ALU.add))
                nc.vector.tensor_scalar(STEPV[:, 2:3], STEPV[:, 7:8], float(D), None, ALU.mult).then_inc(s_stepv, 1)
                dve.wait_ge(s_tabmm, c + 1)
                tab = small_ps[0:1, 64:64 + 4 * STEPS].rearrange("p (k m) -> p k m", k=4)
                nc.vector.tensor_copy(TABP[:, par, :], tab[:, 2, :])
                nc.vector.tensor_copy(TAB[:, par, 2, :], tab[:, 3, :])
                nc.vector.tensor_copy(TAB[:, par, 0:2, :], tab[:, 0:2, :]).then_inc(s_tab, 1)
                return chain["n"] - start

            def permute_tile(t, k):
                tc = t["col"]
                nc.vector.tensor_scalar(PSEL[:, k % 4, :], IOTA[:, 0:P], QRF[:, 1, bass.ds(tc + k, 1)], None, ALU.is_equal)
                nc.vector.tensor_scalar(PVAL[:, k % 4, 0:TC], IOTA[:, 0:TC], QRF[:, 0, bass.ds(tc + k, 1)],
                                        KEYF[:, bass.ds(tc + k, 1)], ALU.is_equal, ALU.mult)
                nc.vector.tensor_scalar(PVAL[:, k % 4, TC:2 * TC], IOTA[:, 0:TC], QRF[:, 0, bass.ds(tc + k, 1)],
                                        EDGE_W[:, bass.ds(t["w"] + k, 1)], ALU.is_equal, ALU.mult).then_inc(s_perm, 1)

            def permute_group(c, g, k):
                done = c * TC + g * U
                if k < 4:
                    if k == 0:
                        dve.wait_ge(s_perm_used, done + 1)
                else:
                    dve.wait_ge(s_perm_used, done + k - 2)
                permute_tile({"col": g * U, "w": c * TC + g * U}, k)

            def wrap_up(c, par):
                start = chain["n"]
                dve.wait_ge(s_perm_used, (c + 1) * TC + 1)
                nc.vector.tensor_copy(SW[:, par, :], perm_ps[:, TC:2 * TC])
                link(nc.vector.tensor_copy(SKEY[:, :], perm_ps[:, 0:TC]))
                nc.vector.tensor_scalar(SDST[:, par, :], SKEY[:, :], 4095, None, ALU.bitwise_and)
                link(nc.vector.tensor_scalar(SHI[:, :], SKEY[:, :], 12, None, ALU.logical_shift_right))
                nc.vector.tensor_copy(SSRC[:, par, :], SHI[:, :]).then_inc(s_sorted, 1)
                return chain["n"] - start

            dve.wait_ge(s_edges, 48)
            dve.wait_ge(s_const, 8)
            link(nc.vector.memset(CX[:, 0:1], 0.0))
            n_sort = sort(0, 0)
            with dve.Fori(0, NG) as g:
                for k in range(U):
                    permute_group(0, g, k)
            n_wrap = wrap_up(0, 0)
            before = chain["n"]
            per_chunk = n_sort + n_wrap

            def load_steps(par, g):
                return [nc.values_load_multi_w_load_instructions(
                    TAB[0:1, par, k, bass.ds(g * U, U)], engines=DVE, min_val=0, max_val=most,
                    skip_runtime_bounds_check_because="from the step table")[1]
                    for k, most in enumerate((TC - 1, NB * P, NB))]

            def step_sel(c, par, g, k, v):
                if k >= 4:
                    dve.wait_ge(s_step, c * STEPS + g * U + k - 3)
                nc.vector.tensor_scalar(SEL[:, k % 4, :], IOTA[:, bass.ds(v[1][k], P)],
                                        SSRC[:, par, bass.ds(v[0][k], 1)], SW[:, par, bass.ds(v[0][k], 1)],
                                        ALU.is_equal, ALU.mult).then_inc(s_sel, 1)

            def step_add(c, g, k, v):
                dve.wait_ge(s_step, c * STEPS + g * U + k + 1)
                if k:
                    dve.wait_ge(s_added, c * STEPS + g * U + k)
                part = SIDE[:, bass.ds(v[2][k], 1), :].rearrange("p a d -> p (a d)")
                nc.vector.tensor_tensor(part, part, step_out(k),
                                        ALU.add).then_inc(s_added, 1)

            def step_group(c, par, g, with_permute, cn=None):
                v = load_steps(par, g)
                for k in range(U):
                    if with_permute:
                        permute_group(cn, g, k)
                    step_sel(c, par, g, k, v)
                    if k >= 2:
                        step_add(c, g, k - 2, v)
                step_add(c, g, U - 2, v)
                step_add(c, g, U - 1, v)
                dve.wait_ge(s_added, c * STEPS + (g + 1) * U)

            def chunk(c, par, more):
                dve.wait_ge(s_tab, c + 1)
                dve.wait_ge(s_sorted, c + 1)
                if more:
                    chain["base"], chain["n"] = before + c * per_chunk, 0
                    sort(c + 1, 1 - par)
                    with dve.Fori(0, NG) as g:
                        step_group(c, par, g, True, c + 1)
                    wrap_up(c + 1, 1 - par)
                else:
                    with dve.Fori(0, NG) as g:
                        step_group(c, par, g, False)
                with dve.Fori(NG, SG) as g:
                    step_group(c, par, g, False)

            with dve.Fori(0, (NCH - 1) // 2) as i:
                chunk(i * 2, 0, True)
                chunk(i * 2 + 1, 1, True)
            chunk(NCH - 1, 0, False)
            chain["base"], chain["n"] = before + (NCH - 1) * per_chunk, 0

            def mix_prod(b, k):
                nc.vector.tensor_tensor(MIX[:, k, 1, :], EGO[:, bass.ds(b, 1), :].rearrange("p a d -> p (a d)"),
                                        SIDE[:, bass.ds(b, 1), :].rearrange("p a d -> p (a d)"), ALU.mult).then_inc(s_mixp, 1)

            def residual(b, kr, n0):
                xb = X[:, bass.ds(b, 1), :].rearrange("p a d -> p (a d)")
                dve.wait_ge(s_relu, b + 1)
                nc.vector.tensor_tensor(RELU[:, kr, :], RELU[:, kr, :], wide_ps[kr][:, :], ALU.max).then_inc(s_leak, 1)
                dve.wait_ge(s_leak, b + 1)
                link(nc.vector.tensor_tensor(xb, xb, RELU[:, kr, 0:D], ALU.add))
                ins = nc.vector.tensor_tensor(xb, xb, RELU[:, kr, D:2 * D], ALU.add)
                ins.then_inc(s_x2, 1)
                dve.wait_ge(s_x2, b + 1)
                nc.vector.bn_stats(STAT[:, bass.ds(b, 1), :].rearrange("p a s -> p (a s)"), xb)

            dve.wait_ge(s_added, NCH * STEPS)
            for b in range(4):
                mix_prod(b, b)
            gbase = chain["base"]
            with dve.Fori(1, NB // 4) as i:
                for k in range(4):
                    dve.wait_ge(s_mixT_mm, i * 4 + k - 3)
                    mix_prod(i * 4 + k, k)
                    chain["base"], chain["n"] = gbase + (i - 1) * 4 + k, 0
                    residual((i - 1) * 4 + k, k % 2, None)
            done = NB - 1 - 4
            chain["base"], chain["n"] = gbase + done, 0
            dve.wait_ge(s_mixT_mm, NB - 4)
            mix_prod(NB - 1, 0)
            for b in range(done, NB):
                residual(b, b % 2, None)
            link(nc.vector.memset(CMPT[:, 0:1], 0.0))

            for b in range(NB):
                last = nc.vector.bn_aggr(MV[:, b, :], STAT[:, b, :])
            link(last)
            nc.vector.tensor_scalar(RS[:, 0, :], MV[:, :, 1], EPS, None, ALU.add).then_inc(s_var2, 1)
            dve.wait_ge(s_std2, 1)
            rsqrt_newton(RS[:, 0, :], RS[:, 1, :], RS[:, 2, :], RS[:, 3, :])
            with dve.Fori(0, XP) as i:
                for k in range(XB):
                    b = i * XB + k
                    last = nc.vector.tensor_scalar(XN2[:, bass.ds(b, 1), :], X[:, bass.ds(b, 1), :],
                                                   MV[:, bass.ds(b, 1), 0:1], RS[:, 2, bass.ds(b, 1)],
                                                   ALU.subtract, ALU.mult)
                last.then_inc(s_xn2, 1)
                dve.wait_ge(s_xn2, i + 1)
                for k in range(XB):
                    b = i * XB + k
                    last = nc.vector.scalar_tensor_tensor(SCR[:, k * D:(k + 1) * D], XN2[:, bass.ds(b, 1), :].rearrange("p a d -> p (a d)"),
                                                          1.0, WRB[:, :], ALU.mult, ALU.mult,
                                                          accum_out=WT[:, bass.ds(b, 1)])
                last.then_inc(s_wt, 1)
                dve.wait_ge(s_wt, i + 1)
            link(nc.vector.tensor_scalar(WT[:, :], WT[:, :], BRB[:, 0:1], None, ALU.add))
            link(nc.vector.tensor_scalar(KF[:, 0, :], NODE[:, :], float(N), None, ALU.is_lt))
            link(nc.vector.tensor_scalar(KF[:, 1, :], KF[:, 0, :], 1.0, BIG, ALU.subtract, ALU.mult))
            link(nc.vector.tensor_tensor(WT[:, :], WT[:, :], KF[:, 0, :], ALU.mult))
            nc.vector.tensor_tensor(WT[:, :], WT[:, :], KF[:, 1, :], ALU.add).then_inc(s_wt, 1)

            dve.wait_ge(s_wt, XP + 1)
            dve.wait_ge(s_wrow, -(-NB // 4))
            link(nc.vector.memset(RANK[:, :, :], 0.0))
            for b in range(NB):
                w = WT[:, b:b + 1]
                if b:
                    nc.vector.tensor_scalar(CMP[:, 0:b * P], WROW[:, 0:b * P], w, 0.0, ALU.is_ge, ALU.add,
                                            accum_out=RANK[:, b, 0:1])
                nc.vector.tensor_scalar(CMP[:, b * P:NP], WROW[:, b * P:NP], w, 0.0, ALU.is_gt, ALU.add,
                                        accum_out=RANK[:, b, 1:2])
                link(nc.vector.scalar_tensor_tensor(CMPT[:, :], WROW[:, b * P:(b + 1) * P], w, BELOW[:, :],
                                                    ALU.is_equal, ALU.mult, accum_out=RANK[:, b, 2:3]))
            link(nc.vector.tensor_reduce(KF[:, 0, :], RANK[:, :, :], AX.X, ALU.add))
            link(nc.vector.tensor_scalar(KF[:, 1, :], KF[:, 0, :], float(KEEP), None, ALU.is_lt))
            link(nc.vector.tensor_tensor_scan(KF[:, 2, :], KF[:, 1, :], KF[:, 1, :], 0.0, ALU.add, ALU.max))
            nc.vector.tensor_scalar(KF[:, 1, :], KF[:, 1, :], -4096.0, 4095.0, ALU.mult, ALU.add).then_inc(s_rank, 1)
            dve.wait_ge(s_rank_mm, 1)
            dve.wait_ge(s_rank, 1)
            link(nc.vector.tensor_scalar(KF[:, 0, :], KF[:, 2, :], small_ps[:, 0:1], None, ALU.add))
            link(nc.vector.tensor_tensor(KI[:, 0, :], KF[:, 0, :], KF[:, 1, :], ALU.add))
            nc.vector.tensor_scalar(KI[:, 1, :], KI[:, 0, :], 7, None, ALU.logical_shift_right)
            link(nc.vector.tensor_scalar(KI[:, 2, :], KI[:, 0, :], P - 1, None, ALU.bitwise_and))
            link(nc.vector.tensor_copy(KQR[:, :, :], KI[:, 1:3, :]))
            for b in range(NB):
                if b >= 4:
                    dve.wait_ge(s_pack_used, b - 3)
                nc.vector.tensor_scalar(PSEL[:, b % 4, :], IOTA[:, 0:P], KQR[:, 1, b:b + 1], None, ALU.is_equal)
                nc.vector.tensor_scalar(PVAL[:, b % 4, 0:QT], IOTA[:, 0:QT], KQR[:, 0, b:b + 1], NODE[:, b:b + 1],
                                        ALU.is_equal, ALU.mult)
                nc.vector.tensor_scalar(PVAL[:, b % 4, QT:2 * QT], IOTA[:, 0:QT], KQR[:, 0, b:b + 1], WT[:, b:b + 1],
                                        ALU.is_equal, ALU.mult).then_inc(s_pack, 1)
            dve.wait_ge(s_pack_used, NB)
            nc.vector.tensor_copy(KEPT[:, :], perm_ps[:, 0:QT])
            nc.vector.tensor_copy(KEPTW[:, :], perm_ps[:, QT:2 * QT])
            link(nc.vector.tensor_scalar(SLOT[:, :], SLOT[:, :], float(KEEP), 2.0 * NP, ALU.is_ge, ALU.mult))
            nc.vector.tensor_tensor(KEPTO[:, :], SLOT[:, :], perm_ps[:, 0:QT], ALU.add).then_inc(s_kept, 1)

            dve.wait_ge(s_kept, 1)
            for q in range(QT):
                s = q % 8
                if q >= 8:
                    dve.wait_ge(s_out, 16 * (q - 7))
                dve.wait_ge(s_y_mm, q + 1)
                dve.wait_ge(s_bases[q % 4], 16 * (q // 4 + 1))
                nc.vector.scalar_tensor_tensor(YOUT[:, s * D:(s + 1) * D], wide_ps[2 + q % 2][:, 0:D],
                                               KEPTW[:, q:q + 1], TBASE[:, s * D:(s + 1) * D],
                                               ALU.mult, ALU.add).then_inc(s_y, 1)

        @block.tensor
        def _(pe):
            pe.wait_ge(s_const, 8)
            def sort(c):
                pe.wait_ge(s_hist, c + 1)
                nc.tensor.matmul(small_ps[:, 0:NB], LOWER[:, :], NCNT[:, :], start=True, stop=False)
                nc.tensor.matmul(small_ps[:, 0:NB], ONES[:, :], CX[:, 0:NB], start=False, stop=True)
                nc.tensor.matmul(small_ps[:, 32:32 + NB + 1], ONES[:, :], CX[:, :], start=True, stop=True).then_inc(s_base, 1)
                pe.wait_ge(s_stepv, c + 1)
                for k in range(4):
                    last = nc.tensor.matmul(small_ps[0:1, 64 + k * STEPS:64 + (k + 1) * STEPS], STEPV[:, k:k + 1],
                                            IDENT[:, 0:STEPS], start=True, stop=True)
                last.then_inc(s_tabmm, 1)

            def permute_tile(c, g, k, start, stop):
                pe.wait_ge(s_perm, c * TC + g * U + k + 1)
                nc.tensor.matmul(perm_ps[:, 0:2 * TC], PSEL[:, k % 4, :], PVAL[:, k % 4, :],
                                 start=start, stop=stop).then_inc(s_perm_used, 1)

            def step_group(c, par, g, gathered, permute_of=None, start=False, stop=False):
                pe.sem_inc(s_pe_seen, 1)
                row = TABP[0:1, par, bass.ds(g * U, U)]
                _, v = nc.values_load_multi_w_load_instructions(
                    row, engines=PE, min_val=0, max_val=(RING - 1) * D, skip_runtime_bounds_check_because="from the step table")
                for k in range(U):
                    if permute_of is not None:
                        permute_tile(permute_of, g, k, start and k == 0, stop and k == U - 1)
                    if gathered:
                        pe.wait_ge(s_gather[k % NS], (c * (TC // NS) + g * (U // NS) + k // NS + 1) * 16)
                    pe.wait_ge(s_sel, c * STEPS + g * U + k + 1)
                    if k >= 4:
                        pe.wait_ge(s_added, c * STEPS + g * U + k - 3)
                    out_ps = step_out(k)
                    nc.tensor.matmul(out_ps, SEL[:, k % 4, :], ROWS[:, bass.ds(v[k], D)],
                                     start=True, stop=True).then_inc(s_step, 1)

            def permutes(c, g, start, stop):
                for k in range(U):
                    permute_tile(c, g, k, start and k == 0, stop and k == U - 1)

            pe.sem_inc(s_perm_used, 1)
            sort(0)
            permutes(0, 0, True, False)
            with pe.Fori(1, NG - 1) as g:
                permutes(0, g, False, False)
            permutes(0, NG - 1, False, True)

            def chunk(c, par, more):
                pe.wait_ge(s_tab, c + 1)
                if more:
                    sort(c + 1)
                    pe.wait_ge(s_sorted, c + 1)
                    step_group(c, par, 0, True, c + 1, start=True)
                    with pe.Fori(1, NG - 1) as g:
                        step_group(c, par, g, True, c + 1)
                    step_group(c, par, NG - 1, True, c + 1, stop=True)
                else:
                    with pe.Fori(0, NG) as g:
                        step_group(c, par, g, True)
                with pe.Fori(NG, SG) as g:
                    step_group(c, par, g, False)

            with pe.Fori(0, (NCH - 1) // 2) as i:
                chunk(i * 2, 0, True)
                chunk(i * 2 + 1, 1, True)
            chunk(NCH - 1, 0, False)

            pe.wait_ge(s_wts, 160)

            def transposes(b, k, first=False):
                pe.wait_ge(s_mixs, b + 1)
                pe.wait_ge(s_mixp, b + 1)
                if not first:
                    pe.wait_ge(s_mixT, b - 1)
                for m in range(2):
                    for h in range(2):
                        last = nc.tensor.transpose(step_ps[k % 2][:, (2 * m + h) * P:(2 * m + h + 1) * P],
                                                   MIX[:, k % 4, m, h * P:(h + 1) * P], IDENT[:, :])
                last.then_inc(s_mixT_mm, 1)

            def layers(b, k, first=False):
                pe.wait_ge(s_mixT, b + 1)
                if not first:
                    pe.wait_ge(s_leak, b - 1)
                for m, wm in enumerate((W1S, W2S)):
                    o = wide_ps[k % 2][:, m * D:(m + 1) * D]
                    for h in range(2):
                        nc.tensor.matmul(o, MIXT[:, k % 2, 2 * m + h, :], wm[:, h, :], start=(h == 0), stop=False)
                    last = nc.tensor.matmul(o, ONES[0:1, :], BROW[0:1, m, :], start=False, stop=True)
                last.then_inc(s_gnn, 1)

            pe.wait_ge(s_added, NCH * STEPS)
            transposes(0, 0, True)
            for b in range(4):
                transposes(b + 1, b + 1, b < 1)
                layers(b, b, b < 2)
            with pe.Fori(1, NB // 4) as i:
                for k in range(4):
                    transposes(i * 4 + k + 1, k + 1)
                    layers(i * 4 + k, k)
            layers(NB - 1, 0)

            pe.wait_ge(s_wt, XP + 1)
            pe.wait_ge(s_leak, NB)
            for i in range(-(-NB // 4)):
                if i >= 4:
                    pe.wait_ge(s_wrow, i - 3)
                for n in range(min(4, NB - 4 * i)):
                    b = 4 * i + n
                    last = nc.tensor.transpose(wide_ps[i % 4][:, n * P:(n + 1) * P],
                                               WT[:, b:b + 1].to_broadcast([P, P]), IDENT[:, :])
                last.then_inc(s_wrow_mm, 1)

            pe.wait_ge(s_rank, 1)
            nc.tensor.matmul(small_ps[:, 0:1], LOWER[:, :], KF[:, 2, NB - 1:NB], start=True, stop=True).then_inc(s_rank_mm, 1)
            for b in range(NB):
                pe.wait_ge(s_pack, b + 1)
                nc.tensor.matmul(perm_ps[:, 0:2 * QT], PSEL[:, b % 4, :], PVAL[:, b % 4, 0:2 * QT],
                                 start=(b == 0), stop=(b == NB - 1)).then_inc(s_pack_used, 1)

            pairs = [(g, j) for g, tiles in enumerate(GROUPS) for j in range(0, len(tiles), 2)]

            def token_transposes(g):
                for pair, (gg, j) in enumerate(pairs):
                    if gg != g:
                        continue
                    if pair >= 2:
                        pe.wait_ge(s_tokT, pair - 1)
                    for n, q in enumerate(GROUPS[g][j:j + 2]):
                        pe.wait_ge(s_tokens[q % 4], 16 * (q // 4 + 1))
                        for h in range(2):
                            last = nc.tensor.transpose(step_ps[pair % 2][:, h * 256 + n * P:h * 256 + (n + 1) * P],
                                                       TOK[:, (q % 8) * D + h * P:(q % 8) * D + (h + 1) * P], IDENT[:, :])
                    last.then_inc(s_tokT_mm, 1)

            token_transposes(0)
            for g, tiles in enumerate(GROUPS):
                n = len(tiles) * P
                tokt = TOKT[:, (g % 2) * 4 * D:(g % 2 + 1) * 4 * D].rearrange("p (h n) -> p h n", h=2)
                pe.wait_ge(s_tokT, sum(1 for gg, _ in pairs if gg <= g))
                for k in range(H // P):
                    at = g * (H // P) + k
                    if at >= 2:
                        pe.wait_ge(s_h, at - 1)
                    for h in range(2):
                        last = nc.tensor.matmul(wide_ps[k % 2][:, 0:n], FW1[:, h, k * P:(k + 1) * P], tokt[:, h, 0:n],
                                                start=(h == 0), stop=(h == 1))
                    last.then_inc(s_h_mm, 1)
                if g + 1 < len(GROUPS):
                    token_transposes(g + 1)
                pe.wait_ge(s_h, (g + 1) * (H // P))
                for q in tiles:
                    if q >= 2:
                        pe.wait_ge(s_y, q - 1)
                    o = wide_ps[2 + q % 2][:, 0:D]
                    for k in range(H // P):
                        nc.tensor.matmul(o, HT[:, k, (q % 4) * P:(q % 4 + 1) * P], FW2[:, k, :], start=(k == 0), stop=False)
                    nc.tensor.matmul(o, ONES[0:1, :], BROW[0:1, 2, :], start=False, stop=True).then_inc(s_y_mm, 1)


_INS = ["x", "src", "dst", "edge_weight", "L0_gnn_W1", "L0_gnn_b1", "L0_gnn_W2", "L0_gnn_b2",
        "L0_ffn_wr", "L0_ffn_br", "L0_ffn_w1", "L0_ffn_b1", "L0_ffn_w2", "L0_ffn_b2"]


def kernel(**inputs):
    import numpy as np
    import concourse.bacc as bacc
    from concourse import mybir as _mybir
    from concourse.bass_utils import run_bass_kernel_spmd

    a = {k: np.ascontiguousarray(np.asarray(inputs[k])) for k in _INS}
    x = np.zeros((NP, D), np.float32)
    x[:N] = a["x"]

    def edges(v, fill):
        w = np.full((NCH * TC * P,), fill, v.dtype)
        w[:E] = v
        return w.reshape(P, NCH * TC)

    arrays = {
        "x": x,
        "src": edges(a["src"].astype(np.int32), NP - 1),
        "dst": edges(a["dst"].astype(np.int32), 0),
        "edge_weight": edges(a["edge_weight"], 0),
        "fb1": np.ascontiguousarray(a["L0_ffn_b1"].reshape(H // P, P).T),
    }
    for k in _INS:
        if k not in arrays and k != "L0_ffn_b1":
            arrays[k] = a[k]
    nc = bacc.Bacc("TRN2", target_bir_lowering=False, num_devices=1)
    ap = {k: nc.dram_tensor(f"in_{k}", v.shape, _mybir.dt.from_np(v.dtype), kind="ExternalInput").ap()
          for k, v in arrays.items()}
    out = nc.dram_tensor("out_rows", (NP, D), _mybir.dt.float32, kind="ExternalOutput").ap()
    build(nc, ap["x"], ap["src"], ap["dst"], ap["edge_weight"], ap["L0_gnn_W1"], ap["L0_gnn_b1"], ap["L0_gnn_W2"],
          ap["L0_gnn_b2"], ap["L0_ffn_wr"], ap["L0_ffn_br"], ap["L0_ffn_w1"], ap["fb1"], ap["L0_ffn_w2"],
          ap["L0_ffn_b2"], out)
    r = run_bass_kernel_spmd(nc, [{f"in_{k}": v for k, v in arrays.items()}], core_ids=[0])
    return r.results[0]["out_rows"][:N]
```

```python
import concourse.bass as bass
from concourse import mybir
from contextlib import ExitStack

P = 128
N = 3125
D = 256
E = 53125
H = 1024
NB = -(-N // P)
NP = NB * P
KEEP = max(1, int(0.5 * N)) - 1
QT = -(-KEEP // P)
NCH = 5
TC = 84
assert NCH * TC * P >= E and TC % 12 == 0 and TC % 2 == 0
STEPS = TC + NB - 1
assert STEPS % 12 == 0 and STEPS <= P
RING = TC // 2
U = 12
HG = U // 2
NS = 6
NG = TC // U
SG = STEPS // U
BG = 3
assert SG == 3 * BG and NG == 2 * BG + 1
EPS = 1e-5
BIG = 3.0e38
XP = 5
XB = NB // XP



def build(nc, x, src, dst, w_edge, W1, b1, W2, b2, wr, br, fw1, fb1, fw2, fb2, out):
    f32 = mybir.dt.float32
    i32 = mybir.dt.int32
    bf16 = mybir.dt.bfloat16
    ALU = mybir.AluOpType
    ACT = mybir.ActivationFunctionType
    AX = mybir.AxisListType
    DVE = [mybir.EngineType.DVE]
    PE = [mybir.EngineType.PE]

    ctx = ExitStack()
    with ctx:
        def sb(name, shape, dt=f32):
            return ctx.enter_context(nc.sbuf_tensor(name, shape, dt))

        def sem(name):
            return ctx.enter_context(nc.semaphore(name))

        ego_rows = nc.dram_tensor("ego_rows", [NP, D], f32, kind="Internal").ap()
        xn2_rows = nc.dram_tensor("xn2_rows", [NP, D], f32, kind="Internal").ap()
        base_rows = nc.dram_tensor("base_rows", [NP, D], f32, kind="Internal").ap()

        X = sb("X", [P, NB, D])
        EGO = sb("EGO", [P, NB, D])
        SIDE = sb("SIDE", [P, NB + 1, D])
        ROWS = sb("ROWS", [P, RING * D])
        EDGE_SRC = sb("EDGE_SRC", [P, NCH * TC], i32)
        EDGE_DST = sb("EDGE_DST", [P, NCH * TC], i32)
        EDGE_W = sb("EDGE_W", [P, NCH * TC])
        OH = sb("OH", [P, NB * TC], bf16)
        CNT = sb("CNT", [P, NB * TC])
        IOTA = sb("IOTA", [P, (NB + 1) * P])
        IDENT = sb("IDENT", [P, P])
        LOWER = sb("LOWER", [P, P])
        BELOW = sb("BELOW", [P, P])
        ONES = sb("ONES", [P, P])
        ONESB = sb("ONESB", [P, 1], bf16)
        PIDX = sb("PIDX", [P, 1])
        W1S = sb("W1S", [P, 2, D])
        W2S = sb("W2S", [P, 2, D])
        BROW = sb("BROW", [1, 3, D])
        FW1 = sb("FW1", [P, 2, H])
        FB1 = sb("FB1", [P, H // P])
        WRB = sb("WRB", [P, D])
        BRB = sb("BRB", [P, 1])
        BLK = sb("BLK", [P, TC], i32)
        POSF = sb("POSF", [P, TC])
        POSI = sb("POSI", [P, TC], i32)
        QR = sb("QR", [P, 2, TC], i32)
        QRF = sb("QRF", [P, 2, TC])
        KEYF = sb("KEYF", [P, TC])
        CX = sb("CX", [P, NB + 1])
        NCNT = sb("NCNT", [P, NB])
        BASE = sb("BASE", [P, NB])
        SM_I = sb("SM_I", [P, 4, NB + 1], i32)
        SM_F = sb("SM_F", [P, 8, NB + 1])
        STEPV = sb("STEPV", [P, 8])
        TAB = sb("TAB", [1, 2, 2, STEPS], i32)
        TABP = sb("TABP", [1, 2, STEPS], i32)
        OHQ = sb("OHQ", [P, 2, HG, TC], bf16)
        PSEL = sb("PSEL", [P, U, P])
        PVAL = sb("PVAL", [P, U, 2 * TC])
        SKEY = sb("SKEY", [P, TC], i32)
        SHI = sb("SHI", [P, TC], i32)
        SDST = sb("SDST", [P, 2, TC], i32)
        SSRC = sb("SSRC", [P, 2, TC])
        SW = sb("SW", [P, 2, TC])
        SEL = sb("SEL", [P, 4, P])
        STAT = sb("STAT", [P, NB, 6])
        MV = sb("MV", [P, NB, 2])
        RS = sb("RS", [P, 4, NB])
        WT = sb("WT", [P, NB])

        perm_ps = ctx.enter_context(nc.psum_tensor("perm_ps", [P, 512], f32))
        step_ps = [ctx.enter_context(nc.psum_tensor(f"step_ps{i}", [P, 512], f32)) for i in range(2)]
        small_ps = ctx.enter_context(nc.psum_tensor("small_ps", [P, 512], f32))
        wide_ps = [ctx.enter_context(nc.psum_tensor(f"wide_ps{i}", [P, 512], f32)) for i in range(4)]

        def step_out(k):
            return (*step_ps, *wide_ps[0:2])[k % 4][:, 0:D]

        s_edges = sem("s_edges")
        s_xin = [sem(f"s_xin{i}") for i in range(XP)]
        s_wts = sem("s_wts")
        s_fw2 = sem("s_fw2")
        s_const = sem("s_const")
        s_pool_seen = sem("s_pool_seen")
        s_pe_seen = sem("s_pe_seen")
        s_pool = sem("s_pool")
        s_var = sem("s_var")
        s_std = sem("s_std")
        s_ego = sem("s_ego")
        s_mixT_mm = sem("s_mixT_mm")
        s_mixT = sem("s_mixT")
        s_ego_dram = sem("s_ego_dram")
        s_dve = sem("s_dve")
        s_hist = sem("s_hist")
        s_base = sem("s_base")
        s_stepv = sem("s_stepv")
        s_tabmm = sem("s_tabmm")
        s_tab = sem("s_tab")
        s_posq = sem("s_posq")
        s_ohq = sem("s_ohq")
        s_pval = sem("s_pval")
        s_abs = sem("s_abs")
        s_perm = sem("s_perm")
        s_perm_used = sem("s_perm_used")
        s_sorted = sem("s_sorted")
        s_gather = [sem(f"s_gather{i}") for i in range(NS)]
        s_sel = sem("s_sel")
        s_step = sem("s_step")
        s_added = sem("s_added")
        s_mixs = sem("s_mixs")
        s_mixp = sem("s_mixp")
        s_gnn = sem("s_gnn")
        s_relu = sem("s_relu")
        s_leak = sem("s_leak")
        s_x2 = sem("s_x2")
        s_var2 = sem("s_var2")
        s_std2 = sem("s_std2")
        s_xn2 = sem("s_xn2")
        s_sum2 = sem("s_sum2")
        s_tok_dram = sem("s_tok_dram")
        s_base_dram = sem("s_base_dram")
        s_wt = sem("s_wt")
        s_wrow_mm = sem("s_wrow_mm")
        s_wrow = sem("s_wrow")
        s_ties = sem("s_ties")
        s_beats = sem("s_beats")
        s_beats_used = sem("s_beats_used")
        s_rrow = sem("s_rrow")
        s_rankT = sem("s_rankT")
        s_rank = sem("s_rank")
        s_rank_mm = sem("s_rank_mm")
        s_pack = sem("s_pack")
        s_pack_used = sem("s_pack_used")
        s_kept = sem("s_kept")
        s_tokens = [sem(f"s_tokens{i}") for i in range(4)]
        s_bases = [sem(f"s_bases{i}") for i in range(4)]
        s_tokT_mm = sem("s_tokT_mm")
        s_tokT = sem("s_tokT")
        s_h_mm = sem("s_h_mm")
        s_h = sem("s_h")
        s_y_mm = sem("s_y_mm")
        s_y = sem("s_y")
        s_out = sem("s_out")

        XN2 = EGO
        BASE2 = SIDE[:, 0:NB, :]
        FW2 = CNT[:, 0:H // P * D].rearrange("p (k n) -> p k n", k=H // P)
        XFLAT = X[:, :, :].rearrange("p b d -> p (b d)")
        WROW = XFLAT[:, 0:NP]
        BEATS = ROWS[:, 0:NP].bitcast(bf16).rearrange("p (k n) -> p k n", k=2)
        RROW = XFLAT[:, NP:2 * NP]
        RB = -(-NP // 512)
        rank_ps = [perm_ps, *step_ps, *wide_ps]
        TOK = ROWS[:, 0:8 * D]
        TOKT = ROWS[:, 8 * D:16 * D]
        HT = ROWS[:, 16 * D:32 * D].rearrange("p (k n) -> p k n", k=H // P)
        TBASE = ROWS[:, 32 * D:40 * D]
        YOUT = XFLAT[:, 0:8 * D]
        MIX = ROWS[:, 0:8 * D].rearrange("p (k m d) -> p k m d", k=4, m=2)
        MIXT = ROWS[:, 8 * D:12 * D].rearrange("p (k a n) -> p k a n", k=2, a=4)
        RELU = ROWS[:, 12 * D:16 * D].rearrange("p (k d) -> p k d", k=2)
        SCR = ROWS[:, 16 * D:(16 + XB) * D]
        CMPT = sb("CMPT", [P, 2, P])
        NODE = sb("NODE", [P, NB])
        SLOT = sb("SLOT", [P, QT])
        KEPT = sb("KEPT", [P, QT], i32)
        KEPTO = sb("KEPTO", [P, QT], i32)
        KEPTW = sb("KEPTW", [P, QT])
        KF = sb("KF", [P, 3, NB])
        KI = sb("KI", [P, 3, NB], i32)
        KQR = sb("KQR", [P, 2, NB])

        GROUPS = [list(range(q, min(q + 4, QT))) for q in range(0, QT, 4)]

        block = ctx.enter_context(nc.Block())

        @block.sync
        def _(sp):
            xv = x.rearrange("(b p) d -> p b d", p=P)
            sp.dma_start(X[:, 0:XB, :], xv[:, 0:XB, :]).then_inc(s_xin[0], 16)
            sp.dma_start(EDGE_SRC[:, :], src).then_inc(s_edges, 16)
            sp.dma_start(EDGE_DST[:, :], dst).then_inc(s_edges, 16)
            sp.dma_start(EDGE_W[:, :], w_edge).then_inc(s_edges, 16)
            for i in range(1, XP):
                sp.dma_start(X[:, i * XB:(i + 1) * XB, :], xv[:, i * XB:(i + 1) * XB, :]).then_inc(s_xin[i], 16)
            sp.dma_start(W1S[:, :, :], W1.rearrange("(k p) n -> p k n", p=P)).then_inc(s_wts, 16)
            sp.dma_start(W2S[:, :, :], W2.rearrange("(k p) n -> p k n", p=P)).then_inc(s_wts, 16)
            sp.dma_start(BROW[:, 0, :], b1.rearrange("(a n) -> a n", a=1)).then_inc(s_wts, 16)
            sp.dma_start(BROW[:, 1, :], b2.rearrange("(a n) -> a n", a=1)).then_inc(s_wts, 16)
            sp.dma_start(BROW[:, 2, :], fb2.rearrange("(a n) -> a n", a=1)).then_inc(s_wts, 16)
            sp.dma_start(FW1[:, :, :], fw1.rearrange("(k p) n -> p k n", p=P)).then_inc(s_wts, 16)
            sp.dma_start(FB1[:, :], fb1).then_inc(s_wts, 16)
            sp.dma_start(WRB[:, :], bass.AP(tensor=wr.tensor, offset=0, ap=[[0, P], [1, D]])).then_inc(s_wts, 16)
            sp.dma_start(BRB[:, :], bass.AP(tensor=br.tensor, offset=0, ap=[[0, P], [1, 1]])).then_inc(s_wts, 16)
            ev = ego_rows.rearrange("(b p) d -> p b d", p=P)
            for i in range(XP):
                sp.wait_ge(s_ego, i + 1)
                sp.dma_start(ev[:, i * XB:(i + 1) * XB, :], EGO[:, i * XB:(i + 1) * XB, :]).then_inc(s_ego_dram, 16)
            sp.wait_ge(s_tab, NCH)
            sp.dma_start(FW2, fw2.rearrange("(k p) n -> p k n", p=P)).then_inc(s_fw2, 16)
            nv = xn2_rows.rearrange("(b p) d -> p b d", p=P)
            ov = out.rearrange("(b p) d -> p b d", p=P)
            bv = base_rows.rearrange("(b p) d -> p b d", p=P)
            for i in range(XP):
                part = slice(i * XB, (i + 1) * XB)
                sp.wait_ge(s_xn2, i + 1)
                sp.dma_start(nv[:, part, :], XN2[:, part, :]).then_inc(s_tok_dram, 16)
                sp.wait_ge(s_sum2, i + 1)
                sp.dma_start(bv[:, part, :], BASE2[:, part, :]).then_inc(s_tok_dram, 16)
                sp.dma_start(ov[:, part, :], BASE2[:, part, :]).then_inc(s_base_dram, 16)
            sp.wait_ge(s_ego_dram, 16 * XP)
            sp.wait_ge(s_tok_dram, 32 * XP)
            sp.wait_ge(s_base_dram, 16 * XP)
            sp.wait_ge(s_out, 16 * QT)

        def mix_sum(pool, b, k):
            pool.tensor_tensor(MIX[:, k, 0, :], EGO[:, bass.ds(b, 1), :].rearrange("p a d -> p (a d)"),
                               SIDE[:, bass.ds(b, 1), :].rearrange("p a d -> p (a d)"), ALU.add).then_inc(s_mixs, 1)

        @block.gpsimd
        def _(pool):
            pool.iota(IOTA[:, :], pattern=[[1, (NB + 1) * P]], base=0, channel_multiplier=0,
                      allow_small_or_imprecise_dtypes=True).then_inc(s_const, 1)
            pool.iota(PIDX[:, :], pattern=[[0, 1]], base=0, channel_multiplier=1,
                      allow_small_or_imprecise_dtypes=True).then_inc(s_const, 1)
            pool.iota(NODE[:, :], pattern=[[P, NB]], base=0, channel_multiplier=1,
                      allow_small_or_imprecise_dtypes=True).then_inc(s_const, 1)
            pool.iota(SLOT[:, :], pattern=[[P, QT]], base=0, channel_multiplier=1,
                      allow_small_or_imprecise_dtypes=True).then_inc(s_const, 1)
            pool.memset(IDENT[:, :], 0.0).then_inc(s_pool, 1)
            pool.memset(ONES[:, :], 1.0).then_inc(s_pool, 1)
            pool.wait_ge(s_pool, 2)
            pool.affine_select(out=IDENT[:, :], in_=IDENT[:, :], compare_op=ALU.not_equal, fill=1.0,
                               base=0, pattern=[[-1, P]], channel_multiplier=1).then_inc(s_const, 1)
            pool.affine_select(out=LOWER[:, :], in_=ONES[:, :], compare_op=ALU.is_gt, fill=0.0,
                               base=0, pattern=[[1, P]], channel_multiplier=-1).then_inc(s_const, 1)
            pool.affine_select(out=BELOW[:, :], in_=ONES[:, :], compare_op=ALU.is_gt, fill=0.0,
                               base=0, pattern=[[-1, P]], channel_multiplier=1).then_inc(s_const, 1)
            pool.memset(SIDE[:, :, :], 0.0).then_inc(s_const, 1)

            def gathers(c, par, first=False):
                pool.wait_ge(s_sorted, c + 1)
                for j in range(TC):
                    if j >= RING:
                        pool.wait_ge(s_step, c * STEPS + j - RING + NB)
                    elif not first:
                        pool.wait_ge(s_step, (c - 1) * STEPS + j + RING + NB)
                    if not first or j >= NS:
                        pool.wait_ge(s_gather[j % NS], (c * (TC // NS) + j // NS) * 16)
                    pool.sem_inc(s_pool_seen, 1)
                    s = j % RING
                    pool.indirect_dma_start(
                        out=ROWS[:, s * D:(s + 1) * D], out_offset=None, in_=ego_rows,
                        in_offset=bass.IndirectOffsetOnAxis(ap=SDST[:, par, j:j + 1], axis=0),
                    ).then_inc(s_gather[j % NS], 16)

            pool.wait_ge(s_ego_dram, 16 * XP)
            gathers(0, 0, first=True)
            with pool.Fori(0, (NCH - 1) // 2) as i:
                gathers(i * 2 + 1, 1)
                gathers(i * 2 + 2, 0)

            pool.wait_ge(s_added, NCH * STEPS)
            for b in range(4):
                mix_sum(pool, b, b)
            with pool.Fori(1, NB // 4) as i:
                for k in range(4):
                    pool.wait_ge(s_mixT_mm, i * 4 + k - 3)
                    mix_sum(pool, i * 4 + k, k)
            pool.wait_ge(s_mixT_mm, NB - 4)
            mix_sum(pool, NB - 1, 0)

            with pool.Fori(0, XP) as i:
                pool.wait_ge(s_xn2, i + 1)
                pool.tensor_tensor(BASE2[:, bass.ds(i * XB, XB), :], X[:, bass.ds(i * XB, XB), :],
                                   XN2[:, bass.ds(i * XB, XB), :], ALU.add).then_inc(s_sum2, 1)

            def store_kept(q):
                pool.wait_ge(s_y, q + 1)
                pool.indirect_dma_start(
                    out=out, out_offset=bass.IndirectOffsetOnAxis(ap=KEPTO[:, q:q + 1], axis=0),
                    in_=YOUT[:, (q % 8) * D:(q % 8 + 1) * D], in_offset=None,
                    bounds_check=NP - 1, oob_is_err=False).then_inc(s_out, 16)

            pool.wait_ge(s_kept, 1)
            pool.wait_ge(s_tok_dram, 32 * XP)
            pool.wait_ge(s_base_dram, 16 * XP)
            for g, tiles in enumerate(GROUPS):
                for q in tiles:
                    s = q % 8
                    if q >= 8:
                        pool.wait_ge(s_tokT_mm, (q - 8) // 2 + 1)
                        pool.wait_ge(s_y, q - 7)
                    if q >= 4:
                        pool.wait_ge(s_tokens[q % 4], 16 * (q // 4))
                        pool.wait_ge(s_bases[q % 4], 16 * (q // 4))
                    pool.indirect_dma_start(
                        out=TOK[:, s * D:(s + 1) * D], out_offset=None, in_=xn2_rows,
                        in_offset=bass.IndirectOffsetOnAxis(ap=KEPT[:, q:q + 1], axis=0),
                    ).then_inc(s_tokens[q % 4], 16)
                    pool.indirect_dma_start(
                        out=TBASE[:, s * D:(s + 1) * D], out_offset=None, in_=base_rows,
                        in_offset=bass.IndirectOffsetOnAxis(ap=KEPT[:, q:q + 1], axis=0),
                    ).then_inc(s_bases[q % 4], 16)
                if g >= 1:
                    for q in GROUPS[g - 1]:
                        store_kept(q)
            for q in GROUPS[-1]:
                store_kept(q)

        @block.scalar
        def _(act):
            for i in range(XP):
                act.wait_ge(s_var, i + 1)
                act.activation(RS[:, 1, i * XB:(i + 1) * XB], RS[:, 0, i * XB:(i + 1) * XB], ACT.Sqrt).then_inc(s_std, 1)
            def permute_half(c, g, h, first=False, values=True):
                n = (c * NG + g) * 2 + h
                if not first:
                    act.wait_ge(s_perm_used, (n - 1) * HG + 1)
                for k in range(h * HG, (h + 1) * HG):
                    last = act.activation(PSEL[:, k, :], IOTA[:, 0:P], ACT.Abs, bias=QRF[:, 1, bass.ds(g * U + k, 1)])
                last.then_inc(s_abs, 1)
                if values:
                    act.wait_ge(s_ohq, n - 2 * NG + 1)
                    for k in range(h * HG, (h + 1) * HG):
                        act.activation(PVAL[:, k, TC:2 * TC], OHQ[:, h, k % HG, :], ACT.Copy,
                                       scale=EDGE_W[:, bass.ds(c * TC + g * U + k, 1)])
                act.wait_ge(s_abs, n + 1)
                act.activation(PSEL[:, h * HG:(h + 1) * HG, :], PSEL[:, h * HG:(h + 1) * HG, :], ACT.Relu,
                               scale=-1.0, bias=1.0).then_inc(s_perm, 1)

            act.wait_ge(s_posq, 1)
            for h in range(2):
                permute_half(0, 0, h, first=True, values=False)
            with act.Fori(1, NG) as g:
                for h in range(2):
                    permute_half(0, g, h, values=False)
            with act.Fori(1, NCH) as c:
                act.wait_ge(s_posq, c + 1)
                with act.Fori(0, NG) as g:
                    for h in range(2):
                        permute_half(c, g, h)

            def copy_mix(b, k, first=False):
                act.wait_ge(s_mixT_mm, b + 1)
                if not first:
                    act.wait_ge(s_gnn, b - 1)
                act.activation(MIXT[:, k % 2, :, :].rearrange("p a n -> p (a n)"), step_ps[k % 2][:, :],
                               ACT.Copy).then_inc(s_mixT, 1)

            def relus(b, k, first=False):
                act.wait_ge(s_gnn, b + 1)
                if not first:
                    act.wait_ge(s_x2, b - 1)
                act.activation(RELU[:, k % 2, :], wide_ps[k % 2][:, :], ACT.Copy, scale=0.01).then_inc(s_relu, 1)

            copy_mix(0, 0, True)
            for b in range(4):
                copy_mix(b + 1, b + 1, b < 1)
                relus(b, b, b < 2)
            with act.Fori(1, NB // 4) as i:
                for k in range(4):
                    copy_mix(i * 4 + k + 1, k + 1)
                    relus(i * 4 + k, k)
            relus(NB - 1, 0)
            act.wait_ge(s_var2, 1)
            act.activation(RS[:, 1, :], RS[:, 0, :], ACT.Sqrt).then_inc(s_std2, 1)
            act.wait_ge(s_sum2, XP)
            for i in range(-(-NB // 4)):
                n = min(4, NB - 4 * i)
                act.wait_ge(s_wrow_mm, i + 1)
                act.activation(WROW[:, i * 512:i * 512 + n * P], wide_ps[i % 4][:, 0:n * P], ACT.Copy).then_inc(s_wrow, 1)
            pair = 0
            for g, tiles in enumerate(GROUPS):
                for j in range(0, len(tiles), 2):
                    n = min(2, len(tiles) - j)
                    act.wait_ge(s_tokT_mm, pair + 1)
                    if g >= 2 and j == 0:
                        act.wait_ge(s_y_mm, GROUPS[g - 2][-1] + 1)
                    tokt = TOKT[:, (g % 2) * 4 * D:(g % 2 + 1) * 4 * D].rearrange("p (h n) -> p h n", h=2)
                    act.activation(tokt[:, :, j * P:(j + n) * P],
                                   step_ps[pair % 2][:, :].rearrange("p (h n) -> p h n", h=2)[:, :, 0:n * P],
                                   ACT.Copy).then_inc(s_tokT, 1)
                    pair += 1
                n = len(tiles) * P
                for k in range(H // P):
                    act.wait_ge(s_h_mm, g * (H // P) + k + 1)
                    if g >= 1 and k == 0:
                        act.wait_ge(s_y_mm, GROUPS[g - 1][-1] + 1)
                    act.activation(HT[:, k, 0:n], wide_ps[k % 2][:, 0:n], ACT.Gelu_apprx_tanh,
                                   bias=FB1[:, k:k + 1]).then_inc(s_h, 1)

        @block.vector
        def _(dve):
            chain = {"base": 0, "n": 0}

            def link(ins):
                chain["n"] += 1
                ins.then_inc(s_dve, 1)
                dve.wait_ge(s_dve, chain["base"] + chain["n"])

            def rsqrt_newton(v, s, y, t):
                link(nc.vector.reciprocal(y, s))
                link(nc.vector.tensor_tensor(t, y, y, ALU.mult))
                link(nc.vector.tensor_tensor(t, t, v, ALU.mult))
                link(nc.vector.tensor_scalar(t, t, -0.5, 1.5, ALU.mult, ALU.add))
                link(nc.vector.tensor_tensor(y, y, t, ALU.mult))

            oh = OH[:, :].rearrange("p (b t) -> p b t", b=NB)
            cnt = CNT[:, :].rearrange("p (b t) -> p b t", b=NB)

            def sort(c, par):
                start = chain["n"]
                e_src = EDGE_SRC[:, bass.ds(c * TC, TC)]
                e_dst = EDGE_DST[:, bass.ds(c * TC, TC)]
                nc.vector.scalar_tensor_tensor(KEYF[:, :], e_src, 4096.0, e_dst, ALU.mult, ALU.add)
                link(nc.vector.tensor_scalar(BLK[:, :], e_src, 7, None, ALU.logical_shift_right))
                link(nc.vector.tensor_tensor(oh, BLK[:, :].unsqueeze(1).to_broadcast([P, NB, TC]),
                                             IOTA[:, 0:NB].unsqueeze(2).to_broadcast([P, NB, TC]), ALU.is_equal))
                link(nc.vector.tensor_tensor_scan(CNT[:, :], OH[:, :], OH[:, :], 0.0, ALU.add, ALU.max))
                link(nc.vector.tensor_copy(CX[:, 1:NB + 1], cnt[:, :, TC - 1]))
                nc.vector.tensor_tensor(NCNT[:, :], CX[:, 1:NB + 1], CX[:, 0:NB], ALU.subtract).then_inc(s_hist, 1)
                dve.wait_ge(s_base, c + 1)
                link(nc.vector.scalar_tensor_tensor(BASE[:, :], small_ps[:, 0:NB], -1.0, CX[:, 0:NB],
                                                    ALU.add, ALU.subtract))
                nc.vector.tensor_copy(SM_F[:, 0, :], small_ps[:, 32:32 + NB + 1])
                link(nc.vector.tensor_copy(SM_I[:, 0, :], small_ps[:, 32:32 + NB + 1]))
                link(nc.vector.tensor_tensor(cnt, cnt, BASE[:, :].unsqueeze(2).to_broadcast([P, NB, TC]), ALU.add))
                link(nc.vector.tensor_tensor(CNT[:, :], CNT[:, :], OH[:, :], ALU.mult))
                link(nc.vector.tensor_reduce(POSF[:, :], cnt.rearrange("p b t -> p t b"), AX.X, ALU.add))
                link(nc.vector.tensor_copy(POSI[:, :], POSF[:, :]))
                nc.vector.tensor_scalar(QR[:, 0, :], POSI[:, :], 7, None, ALU.logical_shift_right)
                link(nc.vector.tensor_scalar(QR[:, 1, :], POSI[:, :], P - 1, None, ALU.bitwise_and))
                nc.vector.tensor_copy(QRF[:, 0, :], QR[:, 0, :])
                nc.vector.tensor_scalar(QRF[:, 1, :], QR[:, 1, :], -1.0, None, ALU.mult).then_inc(s_posq, 1)
                nc.vector.tensor_scalar(SM_I[:, 1, :], SM_I[:, 0, :], 7, None, ALU.logical_shift_right)
                link(nc.vector.tensor_scalar(SM_I[:, 2, :], SM_I[:, 0, :], P - 1, None, ALU.add))
                link(nc.vector.tensor_scalar(SM_I[:, 3, :], SM_I[:, 2, :], 7, None, ALU.logical_shift_right))
                nc.vector.tensor_tensor(SM_F[:, 1, 0:NB], SM_I[:, 3, 1:NB + 1], SM_I[:, 1, 0:NB], ALU.subtract)
                link(nc.vector.tensor_tensor(SM_F[:, 2, 0:NB], SM_F[:, 0, 1:NB + 1], SM_F[:, 0, 0:NB], ALU.is_gt))
                link(nc.vector.tensor_tensor(SM_F[:, 3, 0:NB], SM_F[:, 1, 0:NB], SM_F[:, 2, 0:NB], ALU.mult))
                link(nc.vector.tensor_tensor_scan(SM_F[:, 4, 0:NB], SM_F[:, 3, 0:NB], SM_F[:, 3, 0:NB], 0.0,
                                                  ALU.add, ALU.max))
                link(nc.vector.tensor_tensor(SM_F[:, 5, 0:NB], SM_I[:, 1, 0:NB], SM_F[:, 4, 0:NB], ALU.subtract))
                nc.vector.tensor_tensor(SM_F[:, 6, 0:NB], SM_F[:, 5, 0:NB], SM_F[:, 3, 0:NB], ALU.add)
                link(nc.vector.tensor_scalar(SM_F[:, 7, 0:NB], SM_F[:, 4, 0:NB], PIDX[:, 0:1], 0.0, ALU.is_le, ALU.add,
                                             accum_out=STEPV[:, 3:4]))
                link(nc.vector.scalar_tensor_tensor(SM_F[:, 5, 0:NB], IOTA[:, 0:NB], STEPV[:, 3:4], SM_F[:, 6, 0:NB],
                                                    ALU.is_equal, ALU.mult, accum_out=STEPV[:, 4:5]))
                nc.vector.tensor_copy(STEPV[:, 1:2], STEPV[:, 3:4])
                link(nc.vector.tensor_scalar(STEPV[:, 5:6], STEPV[:, 4:5], PIDX[:, 0:1], None, ALU.add))
                link(nc.vector.tensor_scalar(STEPV[:, 0:1], STEPV[:, 5:6], float(TC - 1), None, ALU.min))
                link(nc.vector.tensor_scalar(STEPV[:, 6:7], STEPV[:, 0:1], float(RING), -float(RING), ALU.is_ge, ALU.mult))
                link(nc.vector.tensor_tensor(STEPV[:, 7:8], STEPV[:, 6:7], STEPV[:, 0:1], ALU.add))
                nc.vector.tensor_scalar(STEPV[:, 2:3], STEPV[:, 7:8], float(D), None, ALU.mult).then_inc(s_stepv, 1)
                dve.wait_ge(s_tabmm, c + 1)
                tab = small_ps[0:1, 64:64 + 3 * STEPS].rearrange("p (k m) -> p k m", k=3)
                nc.vector.tensor_copy(TAB[:, par, :, :], tab[:, 0:2, :])
                nc.vector.tensor_copy(TABP[:, par, :], tab[:, 2, :]).then_inc(s_tab, 1)
                return chain["n"] - start

            def destination_tiles(c, h, slot):
                dve.wait_ge(s_perm, (c * NG) * 2 + h - 1)
                dve.wait_ge(s_pval, (c * NG) * 2 + h - 1)
                nc.vector.tensor_tensor(OHQ[:, slot, :, :], IOTA[:, 0:TC].unsqueeze(1).to_broadcast([P, HG, TC]),
                                        QRF[:, 0, bass.ds(h * HG, HG)].unsqueeze(2).to_broadcast([P, HG, TC]),
                                        ALU.is_equal).then_inc(s_ohq, 1)

            def key_values(c, h, slot):
                n = (c * NG) * 2 + h
                dve.wait_ge(s_ohq, n - 2 * NG + 1)
                dve.wait_ge(s_perm_used, (n - 1) * HG + 1)
                nc.vector.tensor_tensor(PVAL[:, slot * HG:(slot + 1) * HG, 0:TC], OHQ[:, slot, :, :],
                                        KEYF[:, bass.ds(h * HG, HG)].unsqueeze(2).to_broadcast([P, HG, TC]),
                                        ALU.mult).then_inc(s_pval, 1)

            def wrap_up(c, par):
                start = chain["n"]
                dve.wait_ge(s_perm_used, (c + 1) * TC + 1)
                nc.vector.tensor_copy(SW[:, par, :], perm_ps[:, TC:2 * TC])
                link(nc.vector.tensor_copy(SKEY[:, :], perm_ps[:, 0:TC]))
                nc.vector.tensor_scalar(SDST[:, par, :], SKEY[:, :], 4095, None, ALU.bitwise_and)
                link(nc.vector.tensor_scalar(SHI[:, :], SKEY[:, :], 12, None, ALU.logical_shift_right))
                nc.vector.tensor_copy(SSRC[:, par, :], SHI[:, :]).then_inc(s_sorted, 1)
                return chain["n"] - start

            dve.wait_ge(s_edges, 48)
            dve.wait_ge(s_const, 8)
            nc.vector.memset(ONESB[:, :], 1.0)
            link(nc.vector.memset(CX[:, 0:1], 0.0))
            n_sort = sort(0, 0)

            for i in range(XP):
                part = slice(i * XB, (i + 1) * XB)
                dve.wait_ge(s_xin[i], 16)
                for b in range(i * XB, (i + 1) * XB):
                    last = nc.vector.bn_stats(STAT[:, b, :], X[:, b, :])
                link(last)
                for b in range(i * XB, (i + 1) * XB):
                    last = nc.vector.bn_aggr(MV[:, b, :], STAT[:, b, :])
                link(last)
                nc.vector.tensor_scalar(RS[:, 0, part], MV[:, part, 1], EPS, None, ALU.add).then_inc(s_var, 1)
            for i in range(XP):
                part = slice(i * XB, (i + 1) * XB)
                dve.wait_ge(s_std, i + 1)
                rsqrt_newton(RS[:, 0, part], RS[:, 1, part], RS[:, 2, part], RS[:, 3, part])
                for b in range(i * XB, (i + 1) * XB):
                    last = nc.vector.tensor_scalar(EGO[:, b, :], X[:, b, :], MV[:, b, 0:1], RS[:, 2, b:b + 1],
                                                   ALU.subtract, ALU.mult)
                last.then_inc(s_ego, 1)

            def values(g, first=False):
                for h in range(2):
                    if not first:
                        dve.wait_ge(s_perm_used, (g * 2 + h - 1) * HG + 1)
                    for k in range(h * HG, (h + 1) * HG):
                        nc.vector.tensor_scalar(PVAL[:, k, 0:TC], IOTA[:, 0:TC], QRF[:, 0, bass.ds(g * U + k, 1)],
                                                KEYF[:, bass.ds(g * U + k, 1)], ALU.is_equal, ALU.mult)
                        last = nc.vector.tensor_scalar(PVAL[:, k, TC:2 * TC], IOTA[:, 0:TC],
                                                       QRF[:, 0, bass.ds(g * U + k, 1)],
                                                       EDGE_W[:, bass.ds(g * U + k, 1)], ALU.is_equal, ALU.mult)
                    last.then_inc(s_pval, 1)

            values(0, first=True)
            with dve.Fori(1, NG) as g:
                values(g)
            n_wrap = wrap_up(0, 0)
            before = chain["n"]
            per_chunk = n_sort + n_wrap

            def load_steps(par, m):
                return [nc.values_load_multi_w_load_instructions(
                    TAB[0:1, par, k, bass.ds(m, 4)], engines=DVE, min_val=0, max_val=most,
                    skip_runtime_bounds_check_because="from the step table")[1]
                    for k, most in enumerate((TC - 1, NB))]

            def step_sel(m, s, tile, blk, par):
                if s >= 4:
                    dve.wait_ge(s_step, m + s - 3)
                nc.vector.tensor_scalar(SEL[:, s % 4, :], IOTA[:, bass.ds(blk * P, P)],
                                        SSRC[:, par, bass.ds(tile, 1)], SW[:, par, bass.ds(tile, 1)],
                                        ALU.is_equal, ALU.mult).then_inc(s_sel, 1)

            def step_add(m, s, blk):
                dve.wait_ge(s_step, m + s + 1)
                if s:
                    dve.wait_ge(s_added, m + s)
                part = SIDE[:, bass.ds(blk, 1), :].rearrange("p a d -> p (a d)")
                nc.vector.tensor_tensor(part, part, step_out(s), ALU.add).then_inc(s_added, 1)

            def body(c, par, g, tiles_of=None, permuted=0, ends=False, wrap=None):
                m = c * STEPS + g * U
                v = [load_steps(par, g * U)]
                for s in range(BG * U):
                    n, k = divmod(s, U)
                    step_sel(m, s, v[s // 4][0][s % 4], v[s // 4][1][s % 4], par)
                    if s >= 2:
                        step_add(m, s - 2, v[(s - 2) // 4][1][(s - 2) % 4])
                    if s % 4 == 1 and s + 4 < BG * U:
                        v.append(load_steps(par, g * U + s + 3))
                    if s % HG == 1 and s < U * permuted:
                        h = g * 2 + s // HG
                        if s < U * permuted - 2 * HG or not ends:
                            destination_tiles(tiles_of, h + 2, (s // HG) % 2)
                        if s < U * permuted - HG or not ends:
                            key_values(tiles_of, h + 1, (s // HG + 1) % 2)
                    if wrap is not None and s == U:
                        wrap_up(*wrap)
                for s in (BG * U - 2, BG * U - 1):
                    step_add(m, s, v[-1][1][s % 4])
                dve.wait_ge(s_added, m + BG * U)

            def chunk(c, par, more):
                dve.wait_ge(s_tab, c + 1)
                dve.wait_ge(s_sorted, c + 1)
                if more:
                    chain["base"], chain["n"] = before + c * per_chunk, 0
                    sort(c + 1, 1 - par)
                    destination_tiles(c + 1, 0, 0)
                    destination_tiles(c + 1, 1, 1)
                    key_values(c + 1, 0, 0)
                    with dve.Fori(0, 2) as i:
                        body(c, par, i * BG, tiles_of=c + 1, permuted=BG)
                    body(c, par, 2 * BG, tiles_of=c + 1, permuted=1, ends=True, wrap=(c + 1, 1 - par))
                else:
                    with dve.Fori(0, 3) as i:
                        body(c, par, i * BG)

            with dve.Fori(0, (NCH - 1) // 2) as i:
                chunk(i * 2, 0, True)
                chunk(i * 2 + 1, 1, True)
            chunk(NCH - 1, 0, False)
            chain["base"], chain["n"] = before + (NCH - 1) * per_chunk, 0

            def mix_prod(b, k):
                nc.vector.tensor_tensor(MIX[:, k, 1, :], EGO[:, bass.ds(b, 1), :].rearrange("p a d -> p (a d)"),
                                        SIDE[:, bass.ds(b, 1), :].rearrange("p a d -> p (a d)"), ALU.mult).then_inc(s_mixp, 1)

            def residual(b, kr, n0):
                xb = X[:, bass.ds(b, 1), :].rearrange("p a d -> p (a d)")
                dve.wait_ge(s_relu, b + 1)
                nc.vector.tensor_tensor(RELU[:, kr, :], RELU[:, kr, :], wide_ps[kr][:, :], ALU.max).then_inc(s_leak, 1)
                dve.wait_ge(s_leak, b + 1)
                link(nc.vector.tensor_tensor(xb, xb, RELU[:, kr, 0:D], ALU.add))
                ins = nc.vector.tensor_tensor(xb, xb, RELU[:, kr, D:2 * D], ALU.add)
                ins.then_inc(s_x2, 1)
                dve.wait_ge(s_x2, b + 1)
                nc.vector.bn_stats(STAT[:, bass.ds(b, 1), :].rearrange("p a s -> p (a s)"), xb)

            dve.wait_ge(s_added, NCH * STEPS)
            for b in range(4):
                mix_prod(b, b)
            gbase = chain["base"]
            with dve.Fori(1, NB // 4) as i:
                for k in range(4):
                    dve.wait_ge(s_mixT_mm, i * 4 + k - 3)
                    mix_prod(i * 4 + k, k)
                    chain["base"], chain["n"] = gbase + (i - 1) * 4 + k, 0
                    residual((i - 1) * 4 + k, k % 2, None)
            done = NB - 1 - 4
            chain["base"], chain["n"] = gbase + done, 0
            dve.wait_ge(s_mixT_mm, NB - 4)
            mix_prod(NB - 1, 0)
            for b in range(done, NB):
                residual(b, b % 2, None)
            link(nc.vector.memset(CMPT[:, 0, 0:1], 0.0))

            for b in range(NB):
                last = nc.vector.bn_aggr(MV[:, b, :], STAT[:, b, :])
            link(last)
            nc.vector.tensor_scalar(RS[:, 0, :], MV[:, :, 1], EPS, None, ALU.add).then_inc(s_var2, 1)
            dve.wait_ge(s_std2, 1)
            rsqrt_newton(RS[:, 0, :], RS[:, 1, :], RS[:, 2, :], RS[:, 3, :])
            with dve.Fori(0, XP) as i:
                for k in range(XB):
                    b = i * XB + k
                    last = nc.vector.tensor_scalar(XN2[:, bass.ds(b, 1), :], X[:, bass.ds(b, 1), :],
                                                   MV[:, bass.ds(b, 1), 0:1], RS[:, 2, bass.ds(b, 1)],
                                                   ALU.subtract, ALU.mult)
                last.then_inc(s_xn2, 1)
                dve.wait_ge(s_xn2, i + 1)
                for k in range(XB):
                    b = i * XB + k
                    last = nc.vector.scalar_tensor_tensor(SCR[:, k * D:(k + 1) * D], XN2[:, bass.ds(b, 1), :].rearrange("p a d -> p (a d)"),
                                                          1.0, WRB[:, :], ALU.mult, ALU.mult,
                                                          accum_out=WT[:, bass.ds(b, 1)])
                last.then_inc(s_wt, 1)
                dve.wait_ge(s_wt, i + 1)
            link(nc.vector.tensor_scalar(WT[:, :], WT[:, :], BRB[:, 0:1], None, ALU.add))
            link(nc.vector.tensor_scalar(KF[:, 0, :], NODE[:, :], float(N), None, ALU.is_lt))
            link(nc.vector.tensor_scalar(KF[:, 1, :], KF[:, 0, :], 1.0, BIG, ALU.subtract, ALU.mult))
            link(nc.vector.tensor_tensor(WT[:, :], WT[:, :], KF[:, 0, :], ALU.mult))
            nc.vector.tensor_tensor(WT[:, :], WT[:, :], KF[:, 1, :], ALU.add).then_inc(s_wt, 1)

            dve.wait_ge(s_wt, XP + 1)
            dve.wait_ge(s_wrow, -(-NB // 4))
            for b in range(NB):
                w = WT[:, b:b + 1]
                if b >= 2:
                    dve.wait_ge(s_beats_used, b - 1)
                cmp = BEATS[:, b % 2, :]
                own = slice(b * P, (b + 1) * P)
                nc.vector.scalar_tensor_tensor(CMPT[:, b % 2, :], WROW[:, own], w, LOWER[:, :],
                                               ALU.is_equal, ALU.mult).then_inc(s_ties, 1)
                if b:
                    nc.vector.tensor_scalar(cmp[:, 0:b * P], WROW[:, 0:b * P], w, None, ALU.is_lt)
                if b < NB - 1:
                    nc.vector.tensor_scalar(cmp[:, (b + 1) * P:NP], WROW[:, (b + 1) * P:NP], w, None, ALU.is_le)
                dve.wait_ge(s_ties, b + 1)
                nc.vector.scalar_tensor_tensor(cmp[:, own], WROW[:, own], w, CMPT[:, b % 2, :],
                                               ALU.is_lt, ALU.add).then_inc(s_beats, 1)
            dve.wait_ge(s_beats_used, NB)
            for h in range(RB):
                n = min(512, NP - 512 * h)
                last = nc.vector.tensor_copy(RROW[0:1, h * 512:h * 512 + n], rank_ps[h][0:1, 0:n])
            last.then_inc(s_rrow, 1)
            dve.wait_ge(s_rankT, 1)
            link(nc.vector.tensor_copy(KF[:, 0, :], small_ps[:, 0:NB]))
            link(nc.vector.tensor_scalar(KF[:, 1, :], KF[:, 0, :], float(KEEP), None, ALU.is_lt))
            link(nc.vector.tensor_tensor_scan(KF[:, 2, :], KF[:, 1, :], KF[:, 1, :], 0.0, ALU.add, ALU.max))
            nc.vector.tensor_scalar(KF[:, 1, :], KF[:, 1, :], -4096.0, 4095.0, ALU.mult, ALU.add).then_inc(s_rank, 1)
            dve.wait_ge(s_rank_mm, 1)
            dve.wait_ge(s_rank, 1)
            link(nc.vector.tensor_scalar(KF[:, 0, :], KF[:, 2, :], small_ps[:, 0:1], None, ALU.add))
            link(nc.vector.tensor_tensor(KI[:, 0, :], KF[:, 0, :], KF[:, 1, :], ALU.add))
            nc.vector.tensor_scalar(KI[:, 1, :], KI[:, 0, :], 7, None, ALU.logical_shift_right)
            link(nc.vector.tensor_scalar(KI[:, 2, :], KI[:, 0, :], P - 1, None, ALU.bitwise_and))
            link(nc.vector.tensor_copy(KQR[:, :, :], KI[:, 1:3, :]))
            for b in range(NB):
                if b >= 4:
                    dve.wait_ge(s_pack_used, b - 3)
                nc.vector.tensor_scalar(PSEL[:, b % 4, :], IOTA[:, 0:P], KQR[:, 1, b:b + 1], None, ALU.is_equal)
                nc.vector.tensor_scalar(PVAL[:, b % 4, 0:QT], IOTA[:, 0:QT], KQR[:, 0, b:b + 1], NODE[:, b:b + 1],
                                        ALU.is_equal, ALU.mult)
                nc.vector.tensor_scalar(PVAL[:, b % 4, QT:2 * QT], IOTA[:, 0:QT], KQR[:, 0, b:b + 1], WT[:, b:b + 1],
                                        ALU.is_equal, ALU.mult).then_inc(s_pack, 1)
            dve.wait_ge(s_pack_used, NB)
            nc.vector.tensor_copy(KEPT[:, :], perm_ps[:, 0:QT])
            nc.vector.tensor_copy(KEPTW[:, :], perm_ps[:, QT:2 * QT])
            link(nc.vector.tensor_scalar(SLOT[:, :], SLOT[:, :], float(KEEP), 2.0 * NP, ALU.is_ge, ALU.mult))
            nc.vector.tensor_tensor(KEPTO[:, :], SLOT[:, :], perm_ps[:, 0:QT], ALU.add).then_inc(s_kept, 1)

            dve.wait_ge(s_kept, 1)
            for q in range(QT):
                s = q % 8
                if q >= 8:
                    dve.wait_ge(s_out, 16 * (q - 7))
                dve.wait_ge(s_y_mm, q + 1)
                dve.wait_ge(s_bases[q % 4], 16 * (q // 4 + 1))
                nc.vector.scalar_tensor_tensor(YOUT[:, s * D:(s + 1) * D], wide_ps[2 + q % 2][:, 0:D],
                                               KEPTW[:, q:q + 1], TBASE[:, s * D:(s + 1) * D],
                                               ALU.mult, ALU.add).then_inc(s_y, 1)

        @block.tensor
        def _(pe):
            pe.wait_ge(s_const, 8)
            def sort(c):
                pe.wait_ge(s_hist, c + 1)
                nc.tensor.matmul(small_ps[:, 0:NB], LOWER[:, :], NCNT[:, :], start=True, stop=False)
                nc.tensor.matmul(small_ps[:, 0:NB], ONES[:, :], CX[:, 0:NB], start=False, stop=True)
                nc.tensor.matmul(small_ps[:, 32:32 + NB + 1], ONES[:, :], CX[:, :], start=True, stop=True).then_inc(s_base, 1)
                pe.wait_ge(s_stepv, c + 1)
                for k in range(3):
                    last = nc.tensor.matmul(small_ps[0:1, 64 + k * STEPS:64 + (k + 1) * STEPS], STEPV[:, k:k + 1],
                                            IDENT[:, 0:STEPS], start=True, stop=True)
                last.then_inc(s_tabmm, 1)

            def permute_tile(c, g, k, start, stop):
                if k % HG == 0:
                    pe.wait_ge(s_perm, (c * NG + g) * 2 + k // HG + 1)
                    pe.wait_ge(s_pval, (c * NG + g) * 2 + k // HG + 1)
                nc.tensor.matmul(perm_ps[:, 0:2 * TC], PSEL[:, k, :], PVAL[:, k, :],
                                 start=start, stop=stop).then_inc(s_perm_used, 1)

            def load_tiles(par, g):
                return nc.values_load_multi_w_load_instructions(
                    TABP[0:1, par, bass.ds(g * U, U)], engines=PE, min_val=0, max_val=(RING - 1) * D,
                    skip_runtime_bounds_check_because="from the step table")[1]

            def body(c, par, g, gathered=BG, permuted=0, cn=None, start=False, stop=False):
                m = c * STEPS + g * U
                pe.sem_inc(s_pe_seen, 1)
                v = [load_tiles(par, g)]
                for s in range(BG * U):
                    n, k = divmod(s, U)
                    if n < permuted:
                        permute_tile(cn, g + n, k, start and s == 0, stop and s == U * permuted - 1)
                    if k == 4 and n + 1 < BG:
                        pe.sem_inc(s_pe_seen, 1)
                        v.append(load_tiles(par, g + n + 1))
                    if n < gathered:
                        pe.wait_ge(s_gather[k % NS], (c * (TC // NS) + (g + n) * (U // NS) + k // NS + 1) * 16)
                    pe.wait_ge(s_sel, m + s + 1)
                    if s >= 4:
                        pe.wait_ge(s_added, m + s - 3)
                    nc.tensor.matmul(step_out(s), SEL[:, s % 4, :], ROWS[:, bass.ds(v[n][k], D)],
                                     start=True, stop=True).then_inc(s_step, 1)

            def permutes(c, g, start, stop):
                for k in range(U):
                    permute_tile(c, g, k, start and k == 0, stop and k == U - 1)

            pe.sem_inc(s_perm_used, 1)
            sort(0)
            permutes(0, 0, True, False)
            with pe.Fori(1, NG - 1) as g:
                permutes(0, g, False, False)
            permutes(0, NG - 1, False, True)

            def chunk(c, par, more):
                pe.wait_ge(s_tab, c + 1)
                if more:
                    sort(c + 1)
                    pe.wait_ge(s_sorted, c + 1)
                    body(c, par, 0, permuted=BG, cn=c + 1, start=True)
                    body(c, par, BG, permuted=BG, cn=c + 1)
                    body(c, par, 2 * BG, gathered=1, permuted=1, cn=c + 1, stop=True)
                else:
                    with pe.Fori(0, 2) as i:
                        body(c, par, i * BG)
                    body(c, par, 2 * BG, gathered=1)

            with pe.Fori(0, (NCH - 1) // 2) as i:
                chunk(i * 2, 0, True)
                chunk(i * 2 + 1, 1, True)
            chunk(NCH - 1, 0, False)

            pe.wait_ge(s_wts, 144)

            def transposes(b, k, first=False):
                pe.wait_ge(s_mixs, b + 1)
                pe.wait_ge(s_mixp, b + 1)
                if not first:
                    pe.wait_ge(s_mixT, b - 1)
                for m in range(2):
                    for h in range(2):
                        last = nc.tensor.transpose(step_ps[k % 2][:, (2 * m + h) * P:(2 * m + h + 1) * P],
                                                   MIX[:, k % 4, m, h * P:(h + 1) * P], IDENT[:, :])
                last.then_inc(s_mixT_mm, 1)

            def layers(b, k, first=False):
                pe.wait_ge(s_mixT, b + 1)
                if not first:
                    pe.wait_ge(s_leak, b - 1)
                for m, wm in enumerate((W1S, W2S)):
                    o = wide_ps[k % 2][:, m * D:(m + 1) * D]
                    for h in range(2):
                        nc.tensor.matmul(o, MIXT[:, k % 2, 2 * m + h, :], wm[:, h, :], start=(h == 0), stop=False)
                    last = nc.tensor.matmul(o, ONES[0:1, :], BROW[0:1, m, :], start=False, stop=True)
                last.then_inc(s_gnn, 1)

            pe.wait_ge(s_added, NCH * STEPS)
            transposes(0, 0, True)
            for b in range(4):
                transposes(b + 1, b + 1, b < 1)
                layers(b, b, b < 2)
            with pe.Fori(1, NB // 4) as i:
                for k in range(4):
                    transposes(i * 4 + k + 1, k + 1)
                    layers(i * 4 + k, k)
            layers(NB - 1, 0)

            pe.wait_ge(s_wt, XP + 1)
            pe.wait_ge(s_leak, NB)
            for i in range(-(-NB // 4)):
                if i >= 4:
                    pe.wait_ge(s_wrow, i - 3)
                for n in range(min(4, NB - 4 * i)):
                    b = 4 * i + n
                    last = nc.tensor.transpose(wide_ps[i % 4][:, n * P:(n + 1) * P],
                                               WT[:, b:b + 1].to_broadcast([P, P]), IDENT[:, :])
                last.then_inc(s_wrow_mm, 1)

            pe.wait_ge(s_wrow, -(-NB // 4))
            for b in range(NB):
                pe.wait_ge(s_beats, b + 1)
                for h in range(RB):
                    n = min(512, NP - 512 * h)
                    last = nc.tensor.matmul(rank_ps[h][0:1, 0:n], ONESB[:, 0:1], BEATS[:, b % 2, h * 512:h * 512 + n],
                                            start=(b == 0), stop=(b == NB - 1))
                last.then_inc(s_beats_used, 1)
            pe.wait_ge(s_rrow, 1)
            for b in range(NB):
                last = nc.tensor.matmul(small_ps[:, b:b + 1], RROW[0:1, b * P:(b + 1) * P], ONES[0:1, 0:1],
                                        start=True, stop=True)
            last.then_inc(s_rankT, 1)

            pe.wait_ge(s_rank, 1)
            nc.tensor.matmul(small_ps[:, 0:1], LOWER[:, :], KF[:, 2, NB - 1:NB], start=True, stop=True).then_inc(s_rank_mm, 1)
            for b in range(NB):
                pe.wait_ge(s_pack, b + 1)
                nc.tensor.matmul(perm_ps[:, 0:2 * QT], PSEL[:, b % 4, :], PVAL[:, b % 4, 0:2 * QT],
                                 start=(b == 0), stop=(b == NB - 1)).then_inc(s_pack_used, 1)

            pairs = [(g, j) for g, tiles in enumerate(GROUPS) for j in range(0, len(tiles), 2)]

            def token_transposes(g):
                for pair, (gg, j) in enumerate(pairs):
                    if gg != g:
                        continue
                    if pair >= 2:
                        pe.wait_ge(s_tokT, pair - 1)
                    for n, q in enumerate(GROUPS[g][j:j + 2]):
                        pe.wait_ge(s_tokens[q % 4], 16 * (q // 4 + 1))
                        for h in range(2):
                            last = nc.tensor.transpose(step_ps[pair % 2][:, h * 256 + n * P:h * 256 + (n + 1) * P],
                                                       TOK[:, (q % 8) * D + h * P:(q % 8) * D + (h + 1) * P], IDENT[:, :])
                    last.then_inc(s_tokT_mm, 1)

            token_transposes(0)
            pe.wait_ge(s_fw2, 16)
            for g, tiles in enumerate(GROUPS):
                n = len(tiles) * P
                tokt = TOKT[:, (g % 2) * 4 * D:(g % 2 + 1) * 4 * D].rearrange("p (h n) -> p h n", h=2)
                pe.wait_ge(s_tokT, sum(1 for gg, _ in pairs if gg <= g))
                for k in range(H // P):
                    at = g * (H // P) + k
                    if at >= 2:
                        pe.wait_ge(s_h, at - 1)
                    for h in range(2):
                        last = nc.tensor.matmul(wide_ps[k % 2][:, 0:n], FW1[:, h, k * P:(k + 1) * P], tokt[:, h, 0:n],
                                                start=(h == 0), stop=(h == 1))
                    last.then_inc(s_h_mm, 1)
                if g + 1 < len(GROUPS):
                    token_transposes(g + 1)
                pe.wait_ge(s_h, (g + 1) * (H // P))
                for q in tiles:
                    if q >= 2:
                        pe.wait_ge(s_y, q - 1)
                    o = wide_ps[2 + q % 2][:, 0:D]
                    for k in range(H // P):
                        nc.tensor.matmul(o, HT[:, k, (q % 4) * P:(q % 4 + 1) * P], FW2[:, k, :], start=(k == 0), stop=False)
                    nc.tensor.matmul(o, ONES[0:1, :], BROW[0:1, 2, :], start=False, stop=True).then_inc(s_y_mm, 1)


_INS = ["x", "src", "dst", "edge_weight", "L0_gnn_W1", "L0_gnn_b1", "L0_gnn_W2", "L0_gnn_b2",
        "L0_ffn_wr", "L0_ffn_br", "L0_ffn_w1", "L0_ffn_b1", "L0_ffn_w2", "L0_ffn_b2"]


def kernel(**inputs):
    import numpy as np
    import concourse.bacc as bacc
    from concourse import mybir as _mybir
    from concourse.bass_utils import run_bass_kernel_spmd

    a = {k: np.ascontiguousarray(np.asarray(inputs[k])) for k in _INS}
    x = np.zeros((NP, D), np.float32)
    x[:N] = a["x"]

    def edges(v, fill):
        w = np.full((NCH * TC * P,), fill, v.dtype)
        w[:E] = v
        return w.reshape(P, NCH * TC)

    arrays = {
        "x": x,
        "src": edges(a["src"].astype(np.int32), NP - 1),
        "dst": edges(a["dst"].astype(np.int32), 0),
        "edge_weight": edges(a["edge_weight"], 0),
        "fb1": np.ascontiguousarray(a["L0_ffn_b1"].reshape(H // P, P).T),
    }
    for k in _INS:
        if k not in arrays and k != "L0_ffn_b1":
            arrays[k] = a[k]
    nc = bacc.Bacc("TRN2", target_bir_lowering=False, num_devices=1)
    ap = {k: nc.dram_tensor(f"in_{k}", v.shape, _mybir.dt.from_np(v.dtype), kind="ExternalInput").ap()
          for k, v in arrays.items()}
    out = nc.dram_tensor("out_rows", (NP, D), _mybir.dt.float32, kind="ExternalOutput").ap()
    build(nc, ap["x"], ap["src"], ap["dst"], ap["edge_weight"], ap["L0_gnn_W1"], ap["L0_gnn_b1"], ap["L0_gnn_W2"],
          ap["L0_gnn_b2"], ap["L0_ffn_wr"], ap["L0_ffn_br"], ap["L0_ffn_w1"], ap["fb1"], ap["L0_ffn_w2"],
          ap["L0_ffn_b2"], out)
    r = run_bass_kernel_spmd(nc, [{f"in_{k}": v for k, v in arrays.items()}], core_ids=[0])
    return r.results[0]["out_rows"][:N]
```
